# Optimizing a Trainium2 kernel written in Bass

```python
import numpy as np
import jax
import jax.numpy as jnp

def _softmax(x, axis=-1):
    return jax.nn.softmax(x, axis=axis)

def _gelu(x):
    return jax.nn.gelu(x, approximate=True)

def _silu(x):
    return jax.nn.silu(x)

def _sigmoid(x):
    return jax.nn.sigmoid(x)

def _layernorm(x, axis=-1, eps=1e-05):
    m = jnp.mean(x, axis=axis, keepdims=True)
    v = jnp.var(x, axis=axis, keepdims=True)
    return (x - m) / jnp.sqrt(v + eps)

def _scatter_add(tgt, idx, src, axis=0):
    return tgt.at[idx].add(src)

def _segment_sum(src, seg, n):
    return jax.ops.segment_sum(src, seg, n)
kernel_name = 'mk_gnn_resnorm_d4_gnn_r8_01b8b1'

def setup_inputs(seed: int=0):
    np.random.seed(seed)
    _w = jnp.asarray

    def _rec_inputs():
        import jax
        import jax.numpy as jnp
        _gk = jax.random.key(seed)
        x = -0.0002117 + 1 * jax.random.normal(jax.random.fold_in(_gk, 1), (6250, 256), jnp.float32)
        src = jax.random.randint(jax.random.fold_in(_gk, 2), (100000,), 0, 6250, jnp.int32)
        dst = jax.random.randint(jax.random.fold_in(_gk, 3), (100000,), 0, 6250, jnp.int32)
        _o = jnp.argsort(dst, stable=True)
        src = src[_o]
        dst = dst[_o]
        edge_attr_256 = 5.93493e-05 + 1.00006 * jax.random.normal(jax.random.fold_in(_gk, 13), (100000, 256), jnp.float32)
        edge_weight = jax.random.uniform(jax.random.fold_in(_gk, 15), (100000,), jnp.float32, 0.0, 1)
        return (x, src, dst, edge_attr_256, edge_weight)
    x, src, dst, edge_attr_256, edge_weight = _rec_inputs()

    def _L0_gnn_setup():
        import jax, jax.numpy as jnp
        import numpy as np
        N = 12500
        E = 200000
        IN = 256
        HID = 256
        EPS = 1e-05

        def _bn(h, gamma, beta):
            mean = jnp.mean(h, axis=0)
            var = jnp.var(h, axis=0)
            return gamma * (h - mean) * jax.lax.rsqrt(var + EPS) + beta
        key = jax.random.key(seed)
        ks = jax.random.split(key, 12)
        s_in = 1.0 / np.sqrt(IN)
        s_hid = 1.0 / np.sqrt(HID)
        return {'x': jax.random.normal(ks[0], (N, IN), dtype=jnp.float32), 'edge_index': jax.random.randint(ks[1], (2, E), 0, N, dtype=jnp.int64), 'w1': jax.random.uniform(ks[2], (HID, IN), jnp.float32, -s_in, s_in), 'b1': jax.random.uniform(ks[3], (HID,), jnp.float32, -s_in, s_in), 'g1': jnp.ones((HID,), jnp.float32), 'beta1': jnp.zeros((HID,), jnp.float32), 'wr': jax.random.uniform(ks[4], (HID, HID), jnp.float32, -s_hid, s_hid), 'br': jax.random.uniform(ks[5], (HID,), jnp.float32, -s_hid, s_hid), 'wroot': jax.random.uniform(ks[6], (HID, HID), jnp.float32, -s_hid, s_hid), 'w2': jax.random.uniform(ks[7], (IN, HID), jnp.float32, -s_hid, s_hid), 'b2': jax.random.uniform(ks[8], (IN,), jnp.float32, -s_hid, s_hid), 'g2': jnp.ones((IN,), jnp.float32), 'beta2': jnp.zeros((IN,), jnp.float32)}
    _L0_gnn_all = _L0_gnn_setup()
    _L0_gnn_in = {k: v for k, v in _L0_gnn_all.items() if k in ('w1', 'b1', 'g1', 'beta1', 'wr', 'br', 'wroot', 'w2', 'b2', 'g2', 'beta2')}
    del _L0_gnn_all

    def _L1_gnn_setup():
        import jax, jax.numpy as jnp
        import numpy as np
        N_NODES = 12500
        N_EDGES = 400000
        D_IN = 256
        D_OUT = 256
        key = jax.random.key(seed)
        k1, k2, k3, k4, k5, k6 = jax.random.split(key, 6)
        x = jax.random.normal(k1, (N_NODES, D_IN), dtype=jnp.float32)
        edge_val = jax.random.uniform(k2, (N_EDGES,), dtype=jnp.float32)
        stdv = 1.0 / np.sqrt(D_OUT)
        W = jax.random.uniform(k3, (D_IN, D_OUT), dtype=jnp.float32, minval=-stdv, maxval=stdv)
        b = jax.random.uniform(k4, (D_OUT,), dtype=jnp.float32, minval=-stdv, maxval=stdv)
        edge_row = jax.random.randint(k5, (N_EDGES,), 0, N_NODES, dtype=jnp.int32)
        edge_col = jax.random.randint(k6, (N_EDGES,), 0, N_NODES, dtype=jnp.int32)
        return {'x': x, 'edge_val': edge_val, 'W': W, 'b': b, 'edge_row': edge_row, 'edge_col': edge_col}
    _L1_gnn_all = _L1_gnn_setup()
    _L1_gnn_in = {k: v for k, v in _L1_gnn_all.items() if k in ('W', 'b')}
    del _L1_gnn_all

    def _L2_gnn_setup():
        import jax, jax.numpy as jnp
        import numpy as np
        N, E = (6250, 100000)
        IN_C, HID_C, OUT_C = (256, 256, 256)

        def _gcn_prep(edge_index, n_nodes):
            src = jnp.concatenate([edge_index[0], jnp.arange(n_nodes, dtype=edge_index.dtype)])
            dst = jnp.concatenate([edge_index[1], jnp.arange(n_nodes, dtype=edge_index.dtype)])
            deg = jax.ops.segment_sum(jnp.ones_like(dst, dtype=jnp.float32), dst, num_segments=n_nodes)
            deg_inv_sqrt = jnp.where(deg > 0, jax.lax.rsqrt(jnp.maximum(deg, 1.0)), 0.0)
            norm = deg_inv_sqrt[src] * deg_inv_sqrt[dst]
            return (src, dst, norm)

        def _gcn_layer(x, src, dst, norm, W, b, n_nodes):
            h = x @ W
            msg = h[src] * norm[:, None]
            out = jax.ops.segment_sum(msg, dst, num_segments=n_nodes)
            return out + b
        key = jax.random.key(seed)
        ks = jax.random.split(key, 8)
        x_piece = jax.random.normal(ks[0], (N, IN_C), dtype=jnp.float32)
        edge_index_piece = jax.random.randint(ks[1], (2, E), 0, N, dtype=jnp.int64)
        batch = jnp.zeros((N,), dtype=jnp.int64)

        def glorot(k, fan_in, fan_out):
            s = jnp.sqrt(6.0 / (fan_in + fan_out)).astype(jnp.float32)
            return jax.random.uniform(k, (fan_in, fan_out), jnp.float32, -s, s)
        return {'x_piece': x_piece, 'edge_index_piece': edge_index_piece, 'batch': batch, 'W1': glorot(ks[2], IN_C, HID_C), 'b1': jnp.zeros((HID_C,), jnp.float32), 'W2': glorot(ks[3], HID_C, HID_C), 'b2': jnp.zeros((HID_C,), jnp.float32), 'W3': glorot(ks[4], HID_C, OUT_C), 'b3': jnp.zeros((OUT_C,), jnp.float32)}
    _L2_gnn_all = _L2_gnn_setup()
    _L2_gnn_in = {k: v for k, v in _L2_gnn_all.items() if k in ('W1', 'b1', 'W2', 'b2', 'W3', 'b3')}
    del _L2_gnn_all

    def _L3_gnn_setup():
        import jax, jax.numpy as jnp
        import numpy as np
        N, E, D = (6250, 37500, 256)
        BN_EPS = 1e-05

        def _bn(z, gamma, beta, mean, var):
            return (z - mean) * jax.lax.rsqrt(var + BN_EPS) * gamma + beta
        key = jax.random.key(seed)
        ks = jax.random.split(key, 8)
        s = 1.0 / np.sqrt(D)
        return {'x': jax.random.normal(ks[0], (N, D), dtype=jnp.float32), 'edge_index': jax.random.randint(ks[1], (2, E), 0, N, dtype=jnp.int64), 'edge_attr': jax.random.normal(ks[2], (E, D), dtype=jnp.float32), 'W1': jax.random.normal(ks[3], (D, D), dtype=jnp.float32) * s, 'b1': jnp.zeros((D,), jnp.float32), 'W2': jax.random.normal(ks[4], (D, D), dtype=jnp.float32) * s, 'b2': jnp.zeros((D,), jnp.float32), 'bn1_gamma': jnp.ones((D,), jnp.float32), 'bn1_beta': jnp.zeros((D,), jnp.float32), 'bn1_mean': jnp.zeros((D,), jnp.float32), 'bn1_var': jnp.ones((D,), jnp.float32), 'bn2_gamma': jnp.ones((D,), jnp.float32), 'bn2_beta': jnp.zeros((D,), jnp.float32), 'bn2_mean': jnp.zeros((D,), jnp.float32), 'bn2_var': jnp.ones((D,), jnp.float32)}
    _L3_gnn_all = _L3_gnn_setup()
    _L3_gnn_in = {k: v for k, v in _L3_gnn_all.items() if k in ('W1', 'b1', 'W2', 'b2', 'bn1_gamma', 'bn1_beta', 'bn1_mean', 'bn1_var', 'bn2_gamma', 'bn2_beta', 'bn2_mean', 'bn2_var')}
    del _L3_gnn_all
    return {'x': x, 'src': src, 'dst': dst, 'edge_attr_256': edge_attr_256, 'edge_weight': edge_weight, 'L0_gnn_w1': _L0_gnn_in['w1'], 'L0_gnn_b1': _L0_gnn_in['b1'], 'L0_gnn_g1': _L0_gnn_in['g1'], 'L0_gnn_beta1': _L0_gnn_in['beta1'], 'L0_gnn_wr': _L0_gnn_in['wr'], 'L0_gnn_br': _L0_gnn_in['br'], 'L0_gnn_wroot': _L0_gnn_in['wroot'], 'L0_gnn_w2': _L0_gnn_in['w2'], 'L0_gnn_b2': _L0_gnn_in['b2'], 'L0_gnn_g2': _L0_gnn_in['g2'], 'L0_gnn_beta2': _L0_gnn_in['beta2'], 'L1_gnn_W': _L1_gnn_in['W'], 'L1_gnn_b': _L1_gnn_in['b'], 'L2_gnn_W1': _L2_gnn_in['W1'], 'L2_gnn_b1': _L2_gnn_in['b1'], 'L2_gnn_W2': _L2_gnn_in['W2'], 'L2_gnn_b2': _L2_gnn_in['b2'], 'L2_gnn_W3': _L2_gnn_in['W3'], 'L2_gnn_b3': _L2_gnn_in['b3'], 'L3_gnn_W1': _L3_gnn_in['W1'], 'L3_gnn_b1': _L3_gnn_in['b1'], 'L3_gnn_W2': _L3_gnn_in['W2'], 'L3_gnn_b2': _L3_gnn_in['b2'], 'L3_gnn_bn1_gamma': _L3_gnn_in['bn1_gamma'], 'L3_gnn_bn1_beta': _L3_gnn_in['bn1_beta'], 'L3_gnn_bn1_mean': _L3_gnn_in['bn1_mean'], 'L3_gnn_bn1_var': _L3_gnn_in['bn1_var'], 'L3_gnn_bn2_gamma': _L3_gnn_in['bn2_gamma'], 'L3_gnn_bn2_beta': _L3_gnn_in['bn2_beta'], 'L3_gnn_bn2_mean': _L3_gnn_in['bn2_mean'], 'L3_gnn_bn2_var': _L3_gnn_in['bn2_var']}

def reference(x, src, dst, edge_attr_256, edge_weight, L0_gnn_w1, L0_gnn_b1, L0_gnn_g1, L0_gnn_beta1, L0_gnn_wr, L0_gnn_br, L0_gnn_wroot, L0_gnn_w2, L0_gnn_b2, L0_gnn_g2, L0_gnn_beta2, L1_gnn_W, L1_gnn_b, L2_gnn_W1, L2_gnn_b1, L2_gnn_W2, L2_gnn_b2, L2_gnn_W3, L2_gnn_b3, L3_gnn_W1, L3_gnn_b1, L3_gnn_W2, L3_gnn_b2, L3_gnn_bn1_gamma, L3_gnn_bn1_beta, L3_gnn_bn1_mean, L3_gnn_bn1_var, L3_gnn_bn2_gamma, L3_gnn_bn2_beta, L3_gnn_bn2_mean, L3_gnn_bn2_var):
    import jax
    import jax.numpy as jnp

    def _L0_gnn_ref(x, edge_index, w1, b1, g1, beta1, wr, br, wroot, w2, b2, g2, beta2):
        import jax, jax.numpy as jnp
        import numpy as np
        N = 12500
        E = 200000
        IN = 256
        HID = 256
        EPS = 1e-05

        def _bn(h, gamma, beta):
            mean = jnp.mean(h, axis=0)
            var = jnp.var(h, axis=0)
            return gamma * (h - mean) * jax.lax.rsqrt(var + EPS) + beta
        n = x.shape[0]
        h = _bn(x @ w1.T + b1, g1, beta1)
        src, dst = (edge_index[0], edge_index[1])
        agg = jax.ops.segment_sum(h[src], dst, num_segments=n)
        conv = agg @ wr.T + br + h @ wroot.T
        h = jax.nn.gelu(conv, approximate=False)
        out = _bn(h @ w2.T + b2, g2, beta2) + x
        return out

    def _L1_gnn_ref(x, edge_val, W, b, edge_row, edge_col):
        import jax, jax.numpy as jnp
        import numpy as np
        N_NODES = 12500
        N_EDGES = 400000
        D_IN = 256
        D_OUT = 256
        support = jnp.matmul(x, W)
        gathered = support[edge_col] * edge_val[:, None]
        out = jax.ops.segment_sum(gathered, edge_row, num_segments=x.shape[0])
        return out + b

    def _L2_gnn_ref(x_piece, edge_index_piece, batch, W1, b1, W2, b2, W3, b3):
        import jax, jax.numpy as jnp
        import numpy as np
        N, E = (6250, 100000)
        IN_C, HID_C, OUT_C = (256, 256, 256)

        def _gcn_prep(edge_index, n_nodes):
            src = jnp.concatenate([edge_index[0], jnp.arange(n_nodes, dtype=edge_index.dtype)])
            dst = jnp.concatenate([edge_index[1], jnp.arange(n_nodes, dtype=edge_index.dtype)])
            deg = jax.ops.segment_sum(jnp.ones_like(dst, dtype=jnp.float32), dst, num_segments=n_nodes)
            deg_inv_sqrt = jnp.where(deg > 0, jax.lax.rsqrt(jnp.maximum(deg, 1.0)), 0.0)
            norm = deg_inv_sqrt[src] * deg_inv_sqrt[dst]
            return (src, dst, norm)

        def _gcn_layer(x, src, dst, norm, W, b, n_nodes):
            h = x @ W
            msg = h[src] * norm[:, None]
            out = jax.ops.segment_sum(msg, dst, num_segments=n_nodes)
            return out + b
        n_nodes = x_piece.shape[0]
        src, dst, norm = _gcn_prep(edge_index_piece, n_nodes)
        x = _gcn_layer(x_piece, src, dst, norm, W1, b1, n_nodes)
        x = jax.nn.gelu(x)
        x = _gcn_layer(x, src, dst, norm, W2, b2, n_nodes)
        x = jax.nn.gelu(x)
        x = _gcn_layer(x, src, dst, norm, W3, b3, n_nodes)
        return x

    def _L3_gnn_ref(x, edge_index, edge_attr, W1, b1, W2, b2, bn1_gamma, bn1_beta, bn1_mean, bn1_var, bn2_gamma, bn2_beta, bn2_mean, bn2_var):
        import jax, jax.numpy as jnp
        import numpy as np
        N, E, D = (6250, 37500, 256)
        BN_EPS = 1e-05

        def _bn(z, gamma, beta, mean, var):
            return (z - mean) * jax.lax.rsqrt(var + BN_EPS) * gamma + beta
        src, dst = (edge_index[0], edge_index[1])
        msg = jax.nn.relu(x[src] + edge_attr)
        agg = jax.ops.segment_sum(msg, dst, num_segments=x.shape[0])
        conv_out = x + agg
        h = x + conv_out
        f = _bn(h, bn1_gamma, bn1_beta, bn1_mean, bn1_var)
        f = jax.nn.gelu(f @ W1.T + b1, approximate=False)
        f = f @ W2.T + b2
        return _bn(h + f, bn2_gamma, bn2_beta, bn2_mean, bn2_var)
    edge_index = jnp.stack([src, dst])
    batch0 = jnp.zeros((6250,), jnp.int32)
    x = _layernorm(x + _L0_gnn_ref(x, edge_index, L0_gnn_w1, L0_gnn_b1, L0_gnn_g1, L0_gnn_beta1, L0_gnn_wr, L0_gnn_br, L0_gnn_wroot, L0_gnn_w2, L0_gnn_b2, L0_gnn_g2, L0_gnn_beta2), axis=-1)
    x = _layernorm(x + _L1_gnn_ref(x, edge_weight, L1_gnn_W, L1_gnn_b, src, dst), axis=-1)
    x = _layernorm(x + _L2_gnn_ref(x, edge_index, batch0, L2_gnn_W1, L2_gnn_b1, L2_gnn_W2, L2_gnn_b2, L2_gnn_W3, L2_gnn_b3), axis=-1)
    x = _layernorm(x + _L3_gnn_ref(x, edge_index, edge_attr_256, L3_gnn_W1, L3_gnn_b1, L3_gnn_W2, L3_gnn_b2, L3_gnn_bn1_gamma, L3_gnn_bn1_beta, L3_gnn_bn1_mean, L3_gnn_bn1_var, L3_gnn_bn2_gamma, L3_gnn_bn2_beta, L3_gnn_bn2_mean, L3_gnn_bn2_var), axis=-1)
    return x

_drawn_inputs = setup_inputs


def setup_inputs(seed=0):
    import zlib

    import numpy as np

    out = dict(_drawn_inputs(seed))
    spreads = {'L0_gnn_g1': (1.0, 0.2),
     'L0_gnn_beta1': (0.0, 0.1),
     'L0_gnn_g2': (1.0, 0.2),
     'L0_gnn_beta2': (0.0, 0.1),
     'L2_gnn_b1': (0.0, 0.1),
     'L2_gnn_b2': (0.0, 0.1),
     'L2_gnn_b3': (0.0, 0.1),
     'L3_gnn_b1': (0.0, 0.8),
     'L3_gnn_b2': (0.0, 0.676),
     'L3_gnn_bn1_gamma': (1.0, 0.2),
     'L3_gnn_bn1_beta': (0.0, 0.8),
     'L3_gnn_bn1_mean': (0.0, 0.8),
     'L3_gnn_bn1_var': (1.0, 0.2),
     'L3_gnn_bn2_gamma': (1.0, 0.2),
     'L3_gnn_bn2_beta': (0.0, 0.785),
     'L3_gnn_bn2_mean': (0.0, 0.702),
     'L3_gnn_bn2_var': (1.0, 0.2)}
    factors = {'L0_gnn_b1': 8.0, 'L0_gnn_br': 8.0, 'L0_gnn_b2': 8.0}
    for name, (base, spread) in spreads.items():
        noise = np.random.default_rng([zlib.crc32(name.encode()), seed]).standard_normal(out[name].shape)
        drawn = base * np.exp(spread * noise) if base else spread * noise
        out[name] = jnp.asarray(drawn.astype(out[name].dtype))
    for name, factor in factors.items():
        out[name] = (out[name] * factor).astype(out[name].dtype)
    return out
```

```python
from contextlib import ExitStack

import concourse.bass as bass
from concourse import mybir

P = 128
ALU = mybir.AluOpType
ACT = mybir.ActivationFunctionType
F32 = mybir.dt.float32
I32 = mybir.dt.int32
EPS = 1e-5
ds = bass.ds

RING = 16
BATCH = 4
ONEHOTS = 8
LEAD = 4
MSGS = 4
MSG_LEAD = 2
SUMS = 4
REC = 3


def gnn_kernel(nc, a, out):
    N, D = a["x"].shape
    E = a["src"].shape[0]
    T = -(-N // P)
    LAST = N - (T - 1) * P
    NP = T * P
    C = -(-(E + T * (P - 1)) // (P * RING)) * RING
    FE = -(-E // (P * RING)) * RING
    PFULL = E // FE
    REST = E - PFULL * FE
    DH = D // P
    DEGW = D + 1
    NO_TILE = P * (T + 1)
    assert DH == 2 and PFULL == P - 1 and REST > 0 and T % 2 == 1 and T < 64

    rec_dram = {k: nc.dram_tensor(f"records_by_{k}", (P * C + FE, REC), F32).ap() for k in ("dst", "src")}
    tiles_dram = {k: nc.dram_tensor(f"tile_of_chunk_by_{k}", (1, C), I32).ap() for k in ("dst", "src")}
    table = {k: nc.dram_tensor(f"table_{k}", (NP, D), F32).ap() for k in ("h", "x1", "g0", "g1", "g2", "x3")}

    with ExitStack() as ctx:
        def sb(name, shape, dt=F32):
            return ctx.enter_context(nc.sbuf_tensor(name, shape, dt))

        def sem(name):
            return ctx.enter_context(nc.semaphore(name))

        bank = [ctx.enter_context(nc.psum_tensor(f"bank{i}", [P, 512], F32)) for i in range(8)]

        X = sb("X", [P, T * D])
        H = sb("H", [P, T * D])
        acc = sb("acc", [P, T * DEGW])
        rec = sb("rec", [P, C * REC])
        tile_row = sb("tile_row", [1, C], I32)
        ring_mem = sb("ring_mem", [P, RING * DEGW])
        idx_ring = sb("idx_ring", [P, RING], I32)
        eid_ring = sb("eid_ring", [P, RING], I32)
        onehot = sb("onehot", [P, ONEHOTS, P])
        rec_v = rec[:, :].rearrange("p (c w) -> p c w", w=REC)
        G = ring_mem[:, :].rearrange("p (s d) -> p s d", s=RING)
        EA = H[:, 0:RING * D].rearrange("p (s d) -> p s d", s=RING)
        M = H[:, RING * D:(RING + MSGS) * D].rearrange("p (s d) -> p s d", s=MSGS)

        iota_row = sb("iota_row", [P, P])
        ident = sb("ident", [P, P])
        below = sb("below", [P, P])
        upto = sb("upto", [P, P])
        ones = sb("ones", [P, P])

        wt = {k: sb(f"wt_{k}", [P, DH, D]) for k in ("a", "b", "c", "d")}
        pcol = sb("pcol", [P, 9, DH])
        bias = sb("bias", [P, 4, D])
        stats = sb("stats", [P, DH, T * 6])
        ln_stats = sb("ln_stats", [P, 2, 6])
        mv = sb("mv", [P, T * 2])
        std = sb("std", [P, T])
        rstd = sb("rstd", [P, T])
        dis_r = sb("dis_r", [P, T])
        dis = sb("dis", [P, T])
        bn_mv = sb("bn_mv", [P, DH, 2])
        bn_s = sb("bn_s", [P, 4, DH])
        row_mv = sb("row_mv", [P, 2, 2])
        cnt = sb("cnt", [P, 6, 64])
        cnt_i = sb("cnt_i", [P, 2, 64], I32)

        def stage(i):
            return ring_mem[:, 2 * i * D:2 * (i + 1) * D].rearrange("p (s d) -> p s d", s=2)

        stg, fT, hT, gT, nm = (stage(i) for i in range(5))

        def acc_cols(i, n=1, dt=F32):
            part = acc[:, i * FE:(i + n) * FE]
            return part if dt == F32 else part.bitcast(dt)

        ends = {"dst": acc_cols(0, 1, I32), "src": acc_cols(1, 1, I32)}
        weight = acc_cols(2)
        key = acc_cols(3)
        scan = acc_cols(4)
        mask = acc_cols(5)
        tmp_i = acc_cols(6, 1, I32)
        slot_f = acc_cols(7)
        slot_i = {"dst": acc_cols(8, 1, I32), "src": acc_cols(9, 1, I32)}
        rec_e = acc_cols(10, REC)
        chunk_cmp = rec[:, 0:C]
        rec_ev = rec_e.rearrange("p (f w) -> p f w", w=REC)
        scan_i = scan.bitcast(I32)
        mask_i = mask.bitcast(I32)
        idx_stage = idx_ring
        rec_stage = sb("rec_stage", [P, RING, REC])
        rec_stage_flat = rec_stage[:, :, :].rearrange("p s w -> p (s w)")
        assert (10 + REC) * FE <= T * DEGW
        wnat = H[:, 0:4 * DH * D].rearrange("p (q h d) -> p q h d", q=4, h=DH)

        phase_end = sem("phase_end")
        spaced = sem("spaced")
        gathered = [sem(f"gathered{i}") for i in range(RING)]
        ea_in = [sem(f"ea_in{i}") for i in range(RING)]
        scattered = [sem(f"scattered{i}") for i in range(RING // BATCH)]
        staged = sem("staged")
        idx_ready = sem("idx_ready")
        summed = sem("summed")
        onehot_ready = sem("onehot_ready")
        added = sem("added")
        msg_added = sem("msg_added")
        msg_relu = sem("msg_relu")
        vec_chain = sem("vec_chain")
        act_chain = sem("act_chain")
        pool_chain = sem("pool_chain")
        loads = sem("loads")
        edges_in = sem("edges_in")
        stores = sem("stores")
        fills = sem("fills")
        sorts = sem("sorts")
        counts = sem("counts")
        w_in = sem("w_in")
        w_turned = sem("w_turned")
        w_copied = sem("w_copied")
        ln_var = sem("ln_var")
        ln_std = sem("ln_std")
        vars_in = sem("vars_in")

        made = {}

        def psem(phase, what):
            if (phase, what) not in made:
                made[phase, what] = sem(f"{phase}_{what}")
            return made[phase, what]

        block = ctx.enter_context(nc.Block())

        def barrier(eng, k):
            eng.drain().then_inc(phase_end, 1)
            eng.wait_ge(phase_end, 5 * k)

        def hold(eng, sm, value):
            eng.wait_ge(sm, value)
            if not isinstance(value, int):
                eng.sem_inc(spaced, 1)

        def over_tiles(eng, body):
            body(0, 0, False)
            body(1, 1, False)
            with eng.Fori(1, T // 2) as i:
                body(i * 2, 0, True)
                body(i * 2 + 1, 1, True)
            body(T - 1, 0, True)

        def tile(buf, t, width=D, cols=D):
            return buf[:, ds(t * width, cols)]

        AGGS = [("dst", "h", False, True, False), ("src", "x1", True, False, False),
                ("dst", "g0", False, False, False), ("dst", "g1", False, False, False),
                ("dst", "g2", False, False, False), ("dst", "x3", False, False, True)]

        @block.sync
        def _(sp):
            total = {"loads": 0, "stores": 0}

            def load(dst, src, sm=loads, name="loads"):
                sp.dma_start(dst, src).then_inc(sm, 16)
                if name in total:
                    total[name] += 16

            def loaded():
                sp.wait_ge(loads, total["loads"])

            def store(dst, src):
                sp.dma_start(dst, src).then_inc(stores, 16)
                total["stores"] += 16

            def columns(i, name):
                with nc.allow_non_contiguous_dma(reason="256 words"):
                    load(pcol[:, i, :], a[name].rearrange("(h p) -> p h", p=P))

            def bias_row(i, name):
                load(bias[:, i, :], a[name].rearrange("(o d) -> o d", o=1).to_broadcast((P, D)))

            def weights(k, name):
                load(wt[k][:, :, :], a[name].rearrange("(h k) n -> k h n", k=P))

            def natural_weights(names):
                for q, name in enumerate(names):
                    sp.dma_start(wnat[:, q, :, :], a[name].rearrange("(h o) k -> o h k", o=P)).then_inc(w_in, 16)

            def write_table(phase, buf, name):
                def body(t, s, used):
                    sp.wait_ge(psem(phase, "rows"), t + 1)
                    sp.dma_start(table[name][ds(t * P, P), :], tile(buf, t)).then_inc(psem(phase, "written"), 16)
                over_tiles(sp, body)
                sp.wait_ge(psem(phase, "written"), 16 * T)

            def load_records(which):
                load(rec[:, :], rec_dram[which][0:P * C, :].rearrange("(p c) w -> p (c w)", p=P))
                load(tile_row[:, :], tiles_dram[which])
                loaded()

            sp.wait_ge(fills, 1)
            for k in ("dst", "src"):
                sp.dma_start(ends[k][0:PFULL, :], a[k][0:PFULL * FE].rearrange("(p f) -> p f", p=PFULL)).then_inc(edges_in, 16)
                sp.dma_start(ends[k][PFULL:P, 0:REST], a[k][PFULL * FE:E].rearrange("(p f) -> p f", p=1)).then_inc(edges_in, 16)
            sp.dma_start(weight[0:PFULL, :], a["edge_weight"][0:PFULL * FE].rearrange("(p f) -> p f", p=PFULL)).then_inc(edges_in, 16)
            sp.dma_start(weight[PFULL:P, 0:REST], a["edge_weight"][PFULL * FE:E].rearrange("(p f) -> p f", p=1)).then_inc(edges_in, 16)
            natural_weights(("L0_gnn_w1", "L0_gnn_wr", "L0_gnn_wroot", "L0_gnn_w2"))
            for i, name in enumerate(("b1", "g1", "beta1", "br", "b2", "g2", "beta2")):
                columns(i, "L0_gnn_" + name)
            load(X[:, 0:(T - 1) * D].rearrange("p (t d) -> p t d", d=D),
                 a["x"][0:(T - 1) * P, :].rearrange("(t p) d -> p t d", p=P))
            load(X[0:LAST, (T - 1) * D:T * D], a["x"][(T - 1) * P:N, :])
            sp.wait_ge(fills, 2)
            for k in ("dst", "src"):
                store(rec_dram[k][0:P * C, :].rearrange("(p c) w -> p (c w)", p=P), rec[:, :])
            sp.wait_ge(stores, total["stores"])
            sp.sem_inc(psem("sort", "padded"), 1)
            sp.wait_ge(psem("sort", "tiles"), 1)
            store(tiles_dram["dst"], tile_row[:, :])
            sp.wait_ge(stores, total["stores"])
            loaded()
            barrier(sp, 1)

            def h_rows(t, s, used):
                sp.wait_ge(psem("h", "rows"), t + 1)
                sp.dma_start(table["h"][ds(t * P, P), :], nm[:, s, :]).then_inc(psem("h", f"written{s}"), 16)
            over_tiles(sp, h_rows)
            sp.wait_ge(psem("h", "written0"), 16 * (T // 2 + 1))
            sp.wait_ge(psem("h", "written1"), 16 * (T // 2))
            sp.wait_ge(psem("sort", "tiles"), 2)
            store(tiles_dram["src"], tile_row[:, :])
            sp.wait_ge(stores, total["stores"])
            barrier(sp, 2)
            barrier(sp, 3)
            load_records("dst")
            barrier(sp, 4)
            barrier(sp, 5)
            barrier(sp, 6)
            load_records("src")
            weights("a", "L1_gnn_W")
            bias_row(0, "L1_gnn_b")
            loaded()
            write_table("ln0", X, "x1")
            barrier(sp, 7)
            barrier(sp, 8)
            load_records("dst")
            barrier(sp, 9)
            weights("a", "L2_gnn_W1")
            weights("b", "L2_gnn_W2")
            weights("c", "L2_gnn_W3")
            for i in range(3):
                bias_row(i, f"L2_gnn_b{i + 1}")
            loaded()
            write_table("ln1", H, "g0")
            barrier(sp, 10)
            barrier(sp, 11)
            write_table("gcn0", H, "g1")
            barrier(sp, 12)
            barrier(sp, 13)
            write_table("gcn1", H, "g2")
            barrier(sp, 14)
            barrier(sp, 15)
            barrier(sp, 16)
            natural_weights(("L3_gnn_W1", "L3_gnn_W2"))
            bias_row(0, "L3_gnn_b2")
            for i, name in enumerate(("b1", "bn1_gamma", "bn1_beta", "bn1_mean", "bn1_var")):
                columns(i, "L3_gnn_" + name)
            loaded()
            write_table("ln2", X, "x3")
            barrier(sp, 17)
            barrier(sp, 18)
            for i, name in enumerate(("gamma", "beta", "mean", "var")):
                sp.dma_start(H[:, i * D:(i + 1) * D], a["L3_gnn_bn2_" + name].rearrange("(o d) -> o d", o=1)
                             .to_broadcast((P, D))).then_inc(psem("norm2", "in"), 16)
            sp.wait_ge(psem("norm2", "in"), 64)
            barrier(sp, 19)
            barrier(sp, 20)

            def out_rows(t, s, used):
                sp.wait_ge(psem("ln3", "rows"), t + 1)
                if isinstance(t, int) and t == T - 1:
                    sp.dma_start(out[t * P:N, :], X[0:LAST, t * D:(t + 1) * D]).then_inc(psem("ln3", "written"), 16)
                else:
                    sp.dma_start(out[ds(t * P, P), :], tile(X, t)).then_inc(psem("ln3", "written"), 16)
            over_tiles(sp, out_rows)
            sp.wait_ge(psem("ln3", "written"), 16 * T)
            barrier(sp, 21)

        @block.gpsimd
        def _(pool):
            chain = [0]

            def link(ins):
                chain[0] += 1
                ins.then_inc(pool_chain, 1)
                pool.wait_ge(pool_chain, chain[0])

            nc.gpsimd.iota(iota_row[:, :], [[1, P]], 0, channel_multiplier=0, allow_small_or_imprecise_dtypes=True)
            nc.gpsimd.memset(ones[:, :], 1.0)
            link(nc.gpsimd.memset(ident[:, :], 0.0))
            nc.gpsimd.affine_select(out=ident[:, :], in_=ident[:, :], compare_op=ALU.not_equal, fill=1.0,
                                    base=0, pattern=[[-1, P]], channel_multiplier=1).then_inc(counts, 1)
            pool.wait_ge(pool_chain, 1)
            link(nc.gpsimd.affine_select(out=below[:, :], in_=ones[:, :], compare_op=ALU.is_gt, fill=0.0,
                                         base=0, pattern=[[1, P]], channel_multiplier=-1))
            link(nc.gpsimd.affine_select(out=upto[:, :], in_=ones[:, :], compare_op=ALU.is_ge, fill=0.0,
                                         base=0, pattern=[[1, P]], channel_multiplier=-1))
            link(nc.gpsimd.iota(rec_ev[:, :, 2], [[1, FE]], 0, channel_multiplier=FE,
                                allow_small_or_imprecise_dtypes=True))
            pool.sem_inc(counts, 1)

            def sort_iotas(k):
                pool.wait_ge(psem("sort", "cmp_free"), k + 1)
                nc.gpsimd.iota(chunk_cmp, [[1, C]], 0, channel_multiplier=0,
                               allow_small_or_imprecise_dtypes=True).then_inc(psem("sort", "chunk_no"), 1)
                pool.wait_ge(psem("sort", "padded_row"), k + 1)
                nc.gpsimd.iota(slot_f, [[1, FE]], P * C, channel_multiplier=0,
                               allow_small_or_imprecise_dtypes=True).then_inc(psem("sort", "dump_rows"), 1)

            def scatter(k):
                which = ("dst", "src")[k]
                base = 4 * 16 * (FE // RING) * k

                def body(i):
                    for g in range(RING // BATCH):
                        at = i * RING + g * BATCH
                        if not (isinstance(i, int) and i == 0):
                            hold(pool, scattered[g], i * (16 * BATCH) + base)
                        nc.gpsimd.tensor_copy(idx_stage[:, g * BATCH:(g + 1) * BATCH], slot_i[which][:, ds(at, BATCH)])
                        nc.gpsimd.tensor_copy(rec_stage_flat[:, g * BATCH * REC:(g + 1) * BATCH * REC],
                                              rec_e[:, ds(at * REC, BATCH * REC)]).then_inc(staged, 1)
                        hold(pool, staged, i * (RING // BATCH) + g + 1 + k * (FE // BATCH))
                        for j in range(g * BATCH, (g + 1) * BATCH):
                            pool.indirect_dma_start(
                                out=rec_dram[which][:, :], out_offset=bass.IndirectOffsetOnAxis(ap=idx_stage[:, j:j + 1], axis=0),
                                in_=rec_stage[:, j, :], in_offset=None).then_inc(scattered[g], 16)
                body(0)
                with pool.Fori(1, FE // RING) as i:
                    body(i)
                for g in range(RING // BATCH):
                    pool.wait_ge(scattered[g], base + 16 * BATCH * (FE // RING))

            def gather(n):
                which, name, weighted, counted, edges = AGGS[n]
                with pool.Fori(0, C // RING) as i:
                    for s in range(RING):
                        if s % BATCH == 0:
                            hold(pool, idx_ready, i * (RING // BATCH) + s // BATCH + 1 + n * (C // BATCH))
                        pool.indirect_dma_start(
                            out=G[:, s, 0:D], out_offset=None, in_=table[name][:, :],
                            in_offset=bass.IndirectOffsetOnAxis(ap=idx_ring[:, s:s + 1], axis=0)).then_inc(gathered[s], 16)
                        if edges:
                            pool.indirect_dma_start(
                                out=EA[:, s, :], out_offset=None, in_=a["edge_attr_256"][:, :],
                                in_offset=bass.IndirectOffsetOnAxis(ap=eid_ring[:, s:s + 1], axis=0)).then_inc(ea_in[s], 16)

            sort_iotas(0)
            barrier(pool, 1)
            scatter(0)
            sort_iotas(1)
            barrier(pool, 2)
            barrier(pool, 3)
            scatter(1)
            barrier(pool, 4)
            gather(0)
            barrier(pool, 5)
            barrier(pool, 6)
            barrier(pool, 7)
            gather(1)
            barrier(pool, 8)
            barrier(pool, 9)
            barrier(pool, 10)
            gather(2)
            barrier(pool, 11)
            barrier(pool, 12)
            gather(3)
            barrier(pool, 13)
            barrier(pool, 14)
            gather(4)
            barrier(pool, 15)
            barrier(pool, 16)
            barrier(pool, 17)
            gather(5)
            for k in range(18, 22):
                barrier(pool, k)

        @block.tensor
        def _(pe):
            def sum_chunks(n):
                which, name, weighted, counted, edges = AGGS[n]
                width = DEGW if counted else D
                with pe.Fori(0, C // RING) as i:
                    for s in range(RING):
                        c = i * RING + s + n * C
                        pe.wait_ge(onehot_ready, c + 1)
                        if edges:
                            pe.wait_ge(msg_relu, i * RING + s + 1)
                            rows = M[:, s % MSGS, :]
                        else:
                            pe.wait_ge(gathered[s], i * 16 + 16 + n * 16 * (C // RING))
                            rows = G[:, s, 0:width]
                        pe.wait_ge(added, c + 1)
                        pe.matmul(bank[s % SUMS][:, 0:width], onehot[:, s % ONEHOTS, :], rows,
                                  start=True, stop=True).then_inc(summed, 1)

            def turn(phase, src, to, s):
                for h in range(DH):
                    last = pe.transpose(to[:, h * P:(h + 1) * P], src[:, s, h * P:(h + 1) * P], ident[:, :])
                last.then_inc(psem(phase, "turned"), 1)

            def to_features(dst, pairs):
                for o in range(DH):
                    n = 0
                    for wk, val in pairs:
                        for k in range(DH):
                            last = pe.matmul(dst[:, o * P:(o + 1) * P], wk[:, k, o * P:(o + 1) * P],
                                             val[:, k * P:(k + 1) * P], start=(n == 0), stop=(n == DH * len(pairs) - 1))
                            n += 1
                return last

            def to_nodes(dst, wk, val, row=None):
                for k in range(DH):
                    last = pe.matmul(dst[:, 0:D], val[:, k * P:(k + 1) * P], wk[:, k, :], start=(k == 0),
                                     stop=(k == DH - 1 and row is None))
                if row is not None:
                    last = pe.matmul(dst[:, 0:D], ones[0:1, :], row, start=False, stop=True)
                return last

            def sort_counts(k):
                pe.wait_ge(sorts, 3 * k + 1)
                pe.matmul(bank[0][:, 0:T], below[:, :], cnt[:, 0, 0:T], start=True, stop=True)
                pe.matmul(bank[1][:, 0:T], ones[:, :], cnt[:, 0, 0:T], start=True, stop=True)
                pe.matmul(bank[2][0:T, 0:1], cnt[:, 0, 0:T], ones[:, 0:1], start=True, stop=True).then_inc(psem("sort", "mm"), 1)
                pe.wait_ge(sorts, 3 * k + 2)
                pe.matmul(bank[3][0:T, 0:1], upto[0:T, 0:T], cnt[0:T, 5, 0:1], start=True, stop=True).then_inc(psem("sort", "mm"), 1)
                pe.wait_ge(sorts, 3 * k + 3)
                pe.matmul(bank[0][0:1, 0:512], ones[0:T, 0:1], chunk_cmp[0:T, 0:512], start=True, stop=True)
                pe.matmul(bank[1][0:1, 0:C - 512], ones[0:T, 0:1], chunk_cmp[0:T, 512:C], start=True, stop=True).then_inc(psem("sort", "mm"), 1)

            def turn_weights(n, before):
                pe.wait_ge(w_in, 16 * (before + n))
                for q in range(n):
                    if q >= 2:
                        pe.wait_ge(w_copied, before + q - 1)
                    for k in range(DH):
                        for o in range(DH):
                            last = pe.transpose(bank[4 + q % 2][:, k * D + o * P:k * D + (o + 1) * P],
                                                wnat[:, q, o, k * P:(k + 1) * P], ident[:, :])
                    last.then_inc(w_turned, 1)

            pe.wait_ge(counts, 2)
            turn_weights(4, 0)
            sort_counts(0)
            barrier(pe, 1)

            def y_tile(t, s, used):
                pe.wait_ge(psem("y", "staged"), t + 1)
                if used:
                    pe.wait_ge(psem("y", "fT"), t - 1)
                turn("y", stg, bank[4 + s], s)
                pe.wait_ge(psem("y", "fT"), t + 1)
                if used:
                    pe.wait_ge(psem("y", "kept"), t - 1)
                to_features(bank[6 + s], [(wt["a"], fT[:, s, :])]).then_inc(psem("y", "product"), 1)
            over_tiles(pe, y_tile)

            def h_tile(t, s, used):
                pe.wait_ge(psem("h", "scaled"), t + 1)
                if used:
                    pe.wait_ge(psem("h", "rows"), t - 1)
                turn("h", hT, bank[2 + s], s)
            over_tiles(pe, h_tile)
            sort_counts(1)
            barrier(pe, 2)
            barrier(pe, 3)
            barrier(pe, 4)
            sum_chunks(0)
            barrier(pe, 5)

            def conv_tile(t, s, used):
                pe.wait_ge(psem("conv", "staged"), t + 1)
                if used:
                    pe.wait_ge(psem("conv", "fT"), t - 1)
                turn("conv", stg, bank[0 + s], s)
                pe.wait_ge(psem("conv", "hT"), t + 1)
                pe.wait_ge(psem("conv", "fT"), t + 1)
                if used:
                    pe.wait_ge(psem("conv", "gT"), t - 1)
                to_features(bank[2 + s], [(wt["b"], fT[:, s, :]), (wt["c"], hT[:, s, :])]).then_inc(psem("conv", "mid"), 1)
                pe.wait_ge(psem("conv", "gT"), t + 1)
                if used:
                    pe.wait_ge(psem("conv", "kept"), t - 1)
                to_features(bank[4 + s], [(wt["d"], gT[:, s, :])]).then_inc(psem("conv", "product"), 1)
            over_tiles(pe, conv_tile)

            def z_tile(t, s, used):
                pe.wait_ge(psem("z", "scaled"), t + 1)
                if used:
                    pe.wait_ge(psem("z", "v"), t - 1)
                turn("z", hT, bank[6 + s], s)
            over_tiles(pe, z_tile)
            barrier(pe, 6)
            barrier(pe, 7)
            sum_chunks(1)
            barrier(pe, 8)

            def linear(phase, wk, row):
                def body(t, s, used):
                    pe.wait_ge(psem(phase, "staged"), t + 1)
                    if used:
                        pe.wait_ge(psem(phase, "fT"), t - 1)
                    turn(phase, stg, bank[0 + s], s)
                    pe.wait_ge(psem(phase, "fT"), t + 1)
                    if used:
                        pe.wait_ge(psem(phase, "taken"), t - 1)
                    to_nodes(bank[2 + s], wk, fT[:, s, :], row).then_inc(psem(phase, "product"), 1)
                over_tiles(pe, body)

            linear("lin1", wt["a"], bias[0:1, 0, :])
            barrier(pe, 9)
            barrier(pe, 10)
            sum_chunks(2)
            barrier(pe, 11)
            linear("gcn0", wt["a"], None)
            barrier(pe, 12)
            sum_chunks(3)
            barrier(pe, 13)
            linear("gcn1", wt["b"], None)
            barrier(pe, 14)
            sum_chunks(4)
            barrier(pe, 15)
            linear("gcn2", wt["c"], None)
            barrier(pe, 16)
            turn_weights(2, 4)
            barrier(pe, 17)
            sum_chunks(5)
            barrier(pe, 18)
            barrier(pe, 19)

            def ffn_tile(t, s, used):
                pe.wait_ge(psem("ffn", "staged"), t + 1)
                if used:
                    pe.wait_ge(psem("ffn", "fT"), t - 1)
                turn("ffn", stg, bank[0 + s], s)
                pe.wait_ge(psem("ffn", "fT"), t + 1)
                if used:
                    pe.wait_ge(psem("ffn", "gT"), t - 1)
                to_features(bank[2 + s], [(wt["a"], fT[:, s, :])]).then_inc(psem("ffn", "mid"), 1)
                pe.wait_ge(psem("ffn", "gT"), t + 1)
                if used:
                    pe.wait_ge(psem("ffn", "taken"), t - 1)
                to_nodes(bank[4 + s], wt["b"], gT[:, s, :], bias[0:1, 0, :]).then_inc(psem("ffn", "product"), 1)
            over_tiles(pe, ffn_tile)
            barrier(pe, 20)
            barrier(pe, 21)

        @block.scalar
        def _(act):
            def copy_turned(phase, s, t, used, reader, src, scale=None, shift=None):
                act.wait_ge(psem(phase, "turned"), t + 1)
                if used:
                    hold(act, psem(phase, reader), t - 1)
                if scale is None:
                    nc.scalar.copy(fT[:, s, :], src[:, 0:D]).then_inc(psem(phase, "fT"), 1)
                else:
                    for h in range(DH):
                        last = nc.scalar.activation(fT[:, s, h * P:(h + 1) * P], src[:, h * P:(h + 1) * P], ACT.Identity,
                                                    bias=shift[:, h:h + 1], scale=scale[:, h:h + 1])
                    last.then_inc(psem(phase, "fT"), 1)

            def normed(phase, t, s, used, reader, what):
                if used:
                    hold(act, psem(phase, reader), t - 1)
                for h in range(DH):
                    last = nc.scalar.activation(hT[:, s, h * P:(h + 1) * P], H[:, ds(t * D + h * P, P)], ACT.Identity,
                                                bias=bn_s[:, 3, h:h + 1], scale=bn_s[:, 2, h:h + 1])
                last.then_inc(psem(phase, what), 1)

            def root(out_, in_, n):
                act.wait_ge(ln_var, n)
                nc.scalar.activation(out_, in_, ACT.Sqrt).then_inc(ln_std, 1)

            def stage_indices(n):
                which, name, weighted, counted, edges = AGGS[n]

                def stage_batch(i, g):
                    at = i * RING + g * BATCH
                    hold(act, summed, at + BATCH + n * C)
                    last = nc.scalar.copy(idx_ring[:, g * BATCH:(g + 1) * BATCH], rec_v[:, ds(at, BATCH), 0])
                    if edges:
                        last = nc.scalar.copy(eid_ring[:, g * BATCH:(g + 1) * BATCH], rec_v[:, ds(at, BATCH), 2])
                    last.then_inc(idx_ready, 1)

                def relu_batch(i, g):
                    for s in range(g * BATCH, (g + 1) * BATCH):
                        act.wait_ge(msg_added, i * RING + s + 1)
                        nc.scalar.activation(M[:, s % MSGS, :], M[:, s % MSGS, :], ACT.Relu).then_inc(msg_relu, 1)

                if not edges:
                    with act.Fori(0, C // RING) as i:
                        for g in range(RING // BATCH):
                            stage_batch(i, g)
                    return
                for g in range(RING // BATCH - 1):
                    stage_batch(0, g)
                with act.Fori(0, C // RING - 1) as i:
                    for g in range(RING // BATCH):
                        ahead = g + RING // BATCH - 1
                        stage_batch(i + ahead // (RING // BATCH), ahead % (RING // BATCH))
                        relu_batch(i, g)
                i = C // RING - 1
                stage_batch(i, RING // BATCH - 1)
                for g in range(RING // BATCH):
                    relu_batch(i, g)

            def copy_weights(n, before):
                for q in range(n):
                    act.wait_ge(w_turned, before + q + 1)
                    nc.scalar.copy(wt["abcd"[q]][:, :, :].rearrange("p h d -> p (h d)"), bank[4 + q % 2][:, :])\
                      .then_inc(w_copied, 1)

            copy_weights(4, 0)
            barrier(act, 1)

            def y_tile(t, s, used):
                copy_turned("y", s, t, used, "product", bank[4 + s])
                hold(act, psem("y", "product"), t + 1)
                for h in range(DH):
                    last = nc.scalar.activation(H[:, ds(t * D + h * P, P)], bank[6 + s][:, h * P:(h + 1) * P],
                                                ACT.Identity, bias=pcol[:, 0, h:h + 1])
                last.then_inc(psem("y", "kept"), 1)
            over_tiles(act, y_tile)
            root(bn_s[:, 1, :], bn_s[:, 0, :], 1)
            act.wait_ge(vars_in, 1)
            over_tiles(act, lambda t, s, used: normed("h", t, s, used, "turned", "scaled"))
            barrier(act, 2)
            barrier(act, 3)
            barrier(act, 4)
            stage_indices(0)
            barrier(act, 5)

            def conv_tile(t, s, used):
                copy_turned("conv", s, t, used, "mid", bank[0 + s])
                normed("conv", t, s, used, "mid", "hT")
                act.wait_ge(psem("conv", "mid"), t + 1)
                if used:
                    hold(act, psem("conv", "product"), t - 1)
                for h in range(DH):
                    last = nc.scalar.activation(gT[:, s, h * P:(h + 1) * P], bank[2 + s][:, h * P:(h + 1) * P],
                                                ACT.Gelu, bias=pcol[:, 3, h:h + 1])
                last.then_inc(psem("conv", "gT"), 1)
            over_tiles(act, conv_tile)
            root(bn_s[:, 1, :], bn_s[:, 0, :], 2)
            act.wait_ge(vars_in, 2)
            over_tiles(act, lambda t, s, used: normed("z", t, s, used, "turned", "scaled"))
            barrier(act, 6)
            root(std[:, :], rstd[:, :], 3)
            root(dis[:, :], dis_r[:, :], 4)
            barrier(act, 7)
            stage_indices(1)
            barrier(act, 8)
            over_tiles(act, lambda t, s, used: copy_turned("lin1", s, t, used, "product", bank[0 + s]))
            barrier(act, 9)
            root(std[:, :], rstd[:, :], 5)
            barrier(act, 10)
            stage_indices(2)
            barrier(act, 11)

            def gcn_tile(phase):
                def body(t, s, used):
                    copy_turned(phase, s, t, used, "product", bank[0 + s])
                    act.wait_ge(psem(phase, "taken"), t + 1)
                    if used:
                        hold(act, psem(phase, "rows"), t - 1)
                    nc.scalar.activation(hT[:, s, :], gT[:, s, :], ACT.Gelu_apprx_tanh).then_inc(psem(phase, "gelu"), 1)
                return body
            over_tiles(act, gcn_tile("gcn0"))
            barrier(act, 12)
            stage_indices(3)
            barrier(act, 13)
            over_tiles(act, gcn_tile("gcn1"))
            barrier(act, 14)
            stage_indices(4)
            barrier(act, 15)
            over_tiles(act, lambda t, s, used: copy_turned("gcn2", s, t, used, "product", bank[0 + s]))
            barrier(act, 16)
            root(std[:, :], rstd[:, :], 6)
            copy_weights(2, 4)
            barrier(act, 17)
            stage_indices(5)
            barrier(act, 18)
            root(bn_s[:, 1, :], bn_s[:, 0, :], 7)
            root(bias[:, 3, :], H[:, 3 * D:4 * D], 8)
            barrier(act, 19)

            def ffn_tile(t, s, used):
                copy_turned("ffn", s, t, used, "mid", bank[0 + s], bn_s[:, 2, :], bn_s[:, 3, :])
                act.wait_ge(psem("ffn", "mid"), t + 1)
                if used:
                    hold(act, psem("ffn", "product"), t - 1)
                for h in range(DH):
                    last = nc.scalar.activation(gT[:, s, h * P:(h + 1) * P], bank[2 + s][:, h * P:(h + 1) * P],
                                                ACT.Gelu, bias=pcol[:, 0, h:h + 1])
                last.then_inc(psem("ffn", "gT"), 1)
            over_tiles(act, ffn_tile)
            barrier(act, 20)
            root(std[:, :], rstd[:, :], 9)
            barrier(act, 21)

        @block.vector
        def _(dve):
            chain = [0]
            ts, tt, stt = nc.vector.tensor_scalar, nc.vector.tensor_tensor, nc.vector.scalar_tensor_tensor

            def link(ins):
                chain[0] += 1
                ins.then_inc(vec_chain, 1)
                dve.wait_ge(vec_chain, chain[0])

            def sort(k):
                own, other = (("dst", "src"), ("src", "dst"))[k]
                link(ts(tmp_i, ends[own], 7, None, ALU.logical_shift_right))
                link(nc.vector.tensor_copy(key, tmp_i))
                base = chain[0]
                with dve.Fori(0, T) as b:
                    nc.vector.tensor_scalar(mask, key, iota_row[:, ds(b, 1)], 0.0, ALU.is_equal, ALU.add,
                                            accum_out=cnt[:, 0, ds(b, 1)]).then_inc(vec_chain, 1)
                    hold(dve, vec_chain, b + (base + 1))
                chain[0] += T
                nc.vector.drain().then_inc(sorts, 1)
                dve.wait_ge(psem("sort", "mm"), 3 * k + 1)
                link(ts(cnt_i[:, 0, 0:T], bank[1][:, 0:T], float(P - 1), None, ALU.add))
                link(ts(cnt_i[:, 0, 0:T], cnt_i[:, 0, 0:T], 7, None, ALU.logical_shift_right))
                link(nc.vector.tensor_copy(cnt[:, 1, 0:T], cnt_i[:, 0, 0:T]))
                link(ts(cnt_i[0:T, 1, 0:1], bank[2][0:T, 0:1], float(P - 1), None, ALU.add))
                link(ts(cnt_i[0:T, 1, 0:1], cnt_i[0:T, 1, 0:1], 7, None, ALU.logical_shift_right))
                link(nc.vector.tensor_copy(cnt[0:T, 5, 0:1], cnt_i[0:T, 1, 0:1]))
                dve.sem_inc(sorts, 1)
                link(nc.vector.tensor_tensor_scan(cnt[:, 2, 0:T], cnt[:, 1, 0:T], cnt[:, 1, 0:T], 0.0, ALU.add, ALU.max))
                link(tt(cnt[:, 3, 0:T], cnt[:, 2, 0:T], cnt[:, 1, 0:T], ALU.subtract))
                link(stt(cnt[:, 4, 0:T], cnt[:, 3, 0:T], float(P), bank[0][:, 0:T], ALU.mult, ALU.add))
                dve.wait_ge(psem("sort", "mm"), 3 * k + 2)
                link(nc.vector.tensor_copy(cnt[0:T, 5, 1:2], bank[3][0:T, 0:1]))
                dve.sem_inc(psem("sort", "cmp_free"), 1)
                dve.wait_ge(psem("sort", "chunk_no"), k + 1)
                link(ts(chunk_cmp[0:T, :], chunk_cmp[0:T, :], cnt[0:T, 5, 1:2], None, ALU.is_ge))
                dve.sem_inc(sorts, 1)
                link(nc.vector.memset(slot_f, 0.0))
                base = chain[0]
                with dve.Fori(0, T) as b:
                    ts(mask, key, iota_row[:, ds(b, 1)], None, ALU.is_equal).then_inc(vec_chain, 1)
                    hold(dve, vec_chain, b * 3 + (base + 1))
                    nc.vector.tensor_tensor_scan(scan, mask, mask, cnt[:, 4, ds(b, 1)], ALU.add, ALU.max).then_inc(vec_chain, 1)
                    hold(dve, vec_chain, b * 3 + (base + 2))
                    nc.vector.copy_predicated(slot_f, mask_i, scan).then_inc(vec_chain, 1)
                    hold(dve, vec_chain, b * 3 + (base + 3))
                chain[0] += 3 * T
                link(ts(tmp_i, slot_f, -1.0, 0.0, ALU.add, ALU.max))
                dve.sem_inc(psem("sort", "padded_row"), 1)
                link(ts(scan_i, tmp_i, P - 1, None, ALU.bitwise_and))
                link(ts(tmp_i, tmp_i, 7, None, ALU.logical_shift_right))
                link(stt(scan, scan_i, float(C), tmp_i, ALU.mult, ALU.add))
                link(ts(mask, key, float(T), None, ALU.is_lt))
                dve.wait_ge(psem("sort", "dump_rows"), k + 1)
                link(nc.vector.copy_predicated(slot_f, mask_i, scan))
                link(nc.vector.tensor_copy(slot_i[own], slot_f))
                dve.wait_ge(psem("sort", "mm"), 3 * k + 3)
                ts(tile_row[:, 0:512], bank[0][0:1, 0:512], float(T - 1), None, ALU.min)
                link(ts(tile_row[:, 512:C], bank[1][0:1, 0:C - 512], float(T - 1), None, ALU.min))
                dve.sem_inc(psem("sort", "tiles"), 1)

            def records(k):
                own, other = (("dst", "src"), ("src", "dst"))[k]
                nc.vector.tensor_copy(rec_ev[:, :, 0], ends[other])
                link(ts(tmp_i, ends[own], P - 1, None, ALU.bitwise_and))
                link(nc.vector.tensor_copy(rec_ev[:, :, 1], tmp_i))
                if k == 1:
                    link(nc.vector.tensor_copy(rec_ev[:, :, 2], weight))

            def add_chunks(n):
                which, name, weighted, counted, edges = AGGS[n]
                width = DEGW if counted else D

                def one_hot(i, s):
                    c = i * RING + s
                    dve.wait_ge(summed, c + n * C + (RING - ONEHOTS + 1))
                    w_ = rec[:, ds(c * REC + 2, 1)] if weighted else None
                    ts(onehot[:, s % ONEHOTS, :], iota_row[:, :], rec[:, ds(c * REC + 1, 1)], w_, ALU.is_equal,
                       ALU.mult if weighted else ALU.bypass).then_inc(onehot_ready, 1)

                def message(i, s):
                    c = i * RING + s
                    dve.wait_ge(gathered[s], i * 16 + 16 + n * 16 * (C // RING))
                    dve.wait_ge(ea_in[s], i * 16 + 16)
                    dve.wait_ge(summed, c + n * C + (RING - MSGS + 1))
                    tt(M[:, s % MSGS, :], G[:, s, 0:D], EA[:, s, :], ALU.add).then_inc(msg_added, 1)

                def body(i, last):
                    for s in range(RING):
                        c = i * RING + s + n * C
                        t = dve.value_load(tile_row[0:1, ds(i * RING + s, 1)], min_val=0, max_val=T - 1)
                        if not (last and s + LEAD >= RING):
                            one_hot(i + (s + LEAD) // RING, (s + LEAD) % RING)
                        if edges and not (last and s + MSG_LEAD >= RING):
                            message(i + (s + MSG_LEAD) // RING, (s + MSG_LEAD) % RING)
                        dve.wait_ge(summed, c + RING + 1)
                        dve.wait_ge(added, c + SUMS)
                        to = acc[:, ds(t * DEGW, width)]
                        tt(to, bank[s % SUMS][:, 0:width], to, ALU.add).then_inc(added, 1)

                for s in range(LEAD):
                    one_hot(0, s)
                if edges:
                    for s in range(MSG_LEAD):
                        message(0, s)
                with dve.Fori(0, C // RING - 1) as i:
                    body(i, False)
                body(C // RING - 1, True)

            def batch_norm(n, g, b):
                for h in range(DH):
                    link(nc.vector.bn_aggr(bn_mv[:, h, :], stats[:, h, :]))
                fixed_norm(n, bn_mv[:, :, 0], bn_mv[:, :, 1], g, b)

            def fixed_norm(n, mean, var, g, b):
                link(ts(bn_s[:, 0, :], var, EPS, None, ALU.add))
                dve.sem_inc(ln_var, 1)
                dve.wait_ge(ln_std, n)
                link(nc.vector.reciprocal(bn_s[:, 1, :], bn_s[:, 1, :]))
                link(tt(bn_s[:, 2, :], bn_s[:, 1, :], g, ALU.mult))
                link(tt(bn_s[:, 3, :], mean, bn_s[:, 2, :], ALU.mult))
                link(tt(bn_s[:, 3, :], b, bn_s[:, 3, :], ALU.subtract))

            def tile_stats(phase, t):
                n = LAST if isinstance(t, int) and t == T - 1 else P
                for h in range(DH):
                    last = nc.vector.bn_stats(stats[:, h, ds(t * 6, 6)], H[:, ds(t * D + h * P, n)])
                last.then_inc(psem(phase, "stats"), 1)

            def row_stats(phase, t, s):
                hold(dve, psem(phase, "v"), t + 1)
                nc.vector.bn_stats(ln_stats[:, s, :], tile(acc, t, DEGW)).then_inc(psem(phase, "row_stats"), 1)
                hold(dve, psem(phase, "row_stats"), t + 1)
                dve_mean = row_mv[:, s, :]
                nc.vector.bn_aggr(dve_mean, ln_stats[:, s, :]).then_inc(psem(phase, "row_mv"), 1)
                hold(dve, psem(phase, "row_mv"), t + 1)
                ts(mv[:, ds(t * 2, 2)], dve_mean, 1.0, None, ALU.mult).then_inc(psem(phase, "mv"), 1)

            def layer_norm(phase, n, scaled=False):
                mv_v = mv[:, :].rearrange("p (t c) -> p t c", c=2)
                link(ts(rstd[:, :], mv_v[:, :, 1], EPS, None, ALU.add))
                dve.sem_inc(ln_var, 1)
                dve.wait_ge(ln_std, n)
                link(nc.vector.reciprocal(rstd[:, :], std[:, :]))
                if n == 3:
                    link(ts(dis_r[:, :], acc[:, :].rearrange("p (t d) -> p t d", d=DEGW)[:, :, D], 1.0, None, ALU.add))
                    dve.sem_inc(ln_var, 1)
                    dve.wait_ge(ln_std, n + 1)
                    link(nc.vector.reciprocal(dis[:, :], dis[:, :]))

                def body(t, s, used):
                    ins = ts(tile(X, t), tile(acc, t, DEGW), mv[:, ds(t * 2, 1)], rstd[:, ds(t, 1)], ALU.subtract, ALU.mult)
                    if not scaled:
                        ins.then_inc(psem(phase, "rows"), 1)
                        return
                    ins.then_inc(psem(phase, "x"), 1)
                    dve.wait_ge(psem(phase, "x"), t + 1)
                    ts(tile(H, t), tile(X, t), dis[:, ds(t, 1)], None, ALU.mult).then_inc(psem(phase, "rows"), 1)
                over_tiles(dve, body)
                dve.wait_ge(psem(phase, "rows"), T)
                nc.vector.memset(acc[:, :], 0.0)

            nc.vector.memset(ends["dst"], NO_TILE)
            nc.vector.memset(ends["src"], NO_TILE)
            nc.vector.memset(X[:, (T - 1) * D:T * D], 0.0)
            link(nc.vector.memset(weight, 0.0))
            dve.sem_inc(fills, 1)
            link(nc.vector.memset(rec[:, :], 0.0))
            link(nc.vector.memset(rec_v[:, :, 1], -1.0))
            dve.sem_inc(fills, 1)
            dve.wait_ge(counts, 2)
            dve.wait_ge(edges_in, 96)
            dve.wait_ge(psem("sort", "padded"), 1)
            sort(0)
            records(0)
            barrier(dve, 1)

            def y_tile(t, s, used):
                if used:
                    dve.wait_ge(psem("y", "turned"), t - 1)
                ts(stg[:, s, :], tile(X, t), 1.0, None, ALU.mult).then_inc(psem("y", "staged"), 1)
                hold(dve, psem("y", "kept"), t + 1)
                tile_stats("y", t)
            over_tiles(dve, y_tile)
            dve.wait_ge(psem("y", "stats"), T)
            batch_norm(1, pcol[:, 1, :], pcol[:, 2, :])
            dve.sem_inc(vars_in, 1)

            def h_tile(t, s, used):
                dve.wait_ge(psem("h", "turned"), t + 1)
                if used:
                    hold(dve, psem("h", f"written{s}"), (t - s) * 8)
                nc.vector.tensor_copy(nm[:, s, :], bank[2 + s][:, 0:D]).then_inc(psem("h", "rows"), 1)
            over_tiles(dve, h_tile)
            sort(1)
            barrier(dve, 2)
            records(1)
            barrier(dve, 3)
            barrier(dve, 4)
            nc.vector.memset(G[:, :, D], 1.0)
            link(nc.vector.memset(acc[:, :], 0.0))
            dve.sem_inc(summed, RING)
            dve.sem_inc(added, SUMS)
            add_chunks(0)
            barrier(dve, 5)

            def conv_tile(t, s, used):
                if used:
                    dve.wait_ge(psem("conv", "turned"), t - 1)
                ts(stg[:, s, :], tile(acc, t, DEGW), 1.0, None, ALU.mult).then_inc(psem("conv", "staged"), 1)
                dve.wait_ge(psem("conv", "product"), t + 1)
                for h in range(DH):
                    last = ts(H[:, ds(t * D + h * P, P)], bank[4 + s][:, h * P:(h + 1) * P], pcol[:, 4, h:h + 1], None, ALU.add)
                last.then_inc(psem("conv", "kept"), 1)
                hold(dve, psem("conv", "kept"), t + 1)
                tile_stats("conv", t)
            over_tiles(dve, conv_tile)
            dve.wait_ge(psem("conv", "stats"), T)
            batch_norm(2, pcol[:, 5, :], pcol[:, 6, :])
            dve.sem_inc(vars_in, 1)

            def z_tile(t, s, used):
                dve.wait_ge(psem("z", "turned"), t + 1)
                stt(tile(acc, t, DEGW), tile(X, t), 2.0, bank[6 + s][:, 0:D], ALU.mult, ALU.add).then_inc(psem("z", "v"), 1)
                row_stats("z", t, s)
            over_tiles(dve, z_tile)
            barrier(dve, 6)
            layer_norm("ln0", 3)
            barrier(dve, 7)
            add_chunks(1)
            barrier(dve, 8)

            def lin1_tile(t, s, used):
                if used:
                    dve.wait_ge(psem("lin1", "turned"), t - 1)
                ts(stg[:, s, :], tile(acc, t, DEGW), 1.0, None, ALU.mult).then_inc(psem("lin1", "staged"), 1)
                dve.wait_ge(psem("lin1", "product"), t + 1)
                tt(tile(acc, t, DEGW), bank[2 + s][:, 0:D], tile(X, t), ALU.add).then_inc(psem("lin1", "v"), 1)
                hold(dve, psem("lin1", "v"), t + 1)
                dve.sem_inc(psem("lin1", "taken"), 1)
                row_stats("lin1", t, s)
            over_tiles(dve, lin1_tile)
            barrier(dve, 9)
            layer_norm("ln1", 5, scaled=True)
            barrier(dve, 10)
            add_chunks(2)
            barrier(dve, 11)

            def gcn_stage(phase, t, s, used):
                if used:
                    dve.wait_ge(psem(phase, "turned"), t - 1)
                tt(stg[:, s, :], tile(acc, t, DEGW), tile(H, t), ALU.add).then_inc(psem(phase, "staged"), 1)
                dve.wait_ge(psem(phase, "product"), t + 1)

            def gcn_tile(phase, i):
                def body(t, s, used):
                    gcn_stage(phase, t, s, used)
                    if used:
                        dve.wait_ge(psem(phase, "gelu"), t - 1)
                    stt(gT[:, s, :], bank[2 + s][:, 0:D], dis[:, ds(t, 1)], bias[:, i, :], ALU.mult, ALU.add)\
                        .then_inc(psem(phase, "taken"), 1)
                    dve.wait_ge(psem(phase, "gelu"), t + 1)
                    ts(tile(H, t), hT[:, s, :], dis[:, ds(t, 1)], None, ALU.mult).then_inc(psem(phase, "rows"), 1)
                return body

            over_tiles(dve, gcn_tile("gcn0", 0))
            link(nc.vector.memset(acc[:, :], 0.0))
            barrier(dve, 12)
            add_chunks(3)
            barrier(dve, 13)
            over_tiles(dve, gcn_tile("gcn1", 1))
            link(nc.vector.memset(acc[:, :], 0.0))
            barrier(dve, 14)
            add_chunks(4)
            barrier(dve, 15)

            def gcn2_tile(t, s, used):
                gcn_stage("gcn2", t, s, used)
                if used:
                    dve.wait_ge(psem("gcn2", "v"), t - 1)
                stt(gT[:, s, :], bank[2 + s][:, 0:D], dis[:, ds(t, 1)], bias[:, 2, :], ALU.mult, ALU.add)\
                    .then_inc(psem("gcn2", "taken"), 1)
                dve.wait_ge(psem("gcn2", "taken"), t + 1)
                tt(tile(acc, t, DEGW), gT[:, s, :], tile(X, t), ALU.add).then_inc(psem("gcn2", "v"), 1)
                row_stats("gcn2", t, s)
            over_tiles(dve, gcn2_tile)
            barrier(dve, 16)
            layer_norm("ln2", 6)
            barrier(dve, 17)
            add_chunks(5)
            barrier(dve, 18)
            fixed_norm(7, pcol[:, 3, :], pcol[:, 4, :], pcol[:, 1, :], pcol[:, 2, :])
            dve.wait_ge(psem("norm2", "in"), 16 * 4)
            link(ts(H[:, 3 * D:4 * D], H[:, 3 * D:4 * D], EPS, None, ALU.add))
            dve.sem_inc(ln_var, 1)
            dve.wait_ge(ln_std, 8)
            link(nc.vector.reciprocal(bias[:, 3, :], bias[:, 3, :]))
            link(tt(bias[:, 1, :], bias[:, 3, :], H[:, 0:D], ALU.mult))
            link(tt(bias[:, 2, :], H[:, 2 * D:3 * D], bias[:, 1, :], ALU.mult))
            link(tt(bias[:, 2, :], H[:, D:2 * D], bias[:, 2, :], ALU.subtract))
            barrier(dve, 19)

            def ffn_tile(t, s, used):
                if used:
                    dve.wait_ge(psem("ffn", "turned"), t - 1)
                    dve.wait_ge(psem("ffn", "taken"), t - 1)
                stt(stg[:, s, :], tile(X, t), 2.0, tile(acc, t, DEGW), ALU.mult, ALU.add).then_inc(psem("ffn", "staged"), 1)
                dve.wait_ge(psem("ffn", "product"), t + 1)
                dve.wait_ge(psem("ffn", "staged"), t + 1)
                tt(nm[:, s, :], bank[4 + s][:, 0:D], stg[:, s, :], ALU.add).then_inc(psem("ffn", "taken"), 1)
                dve.wait_ge(psem("ffn", "taken"), t + 1)
                tt(nm[:, s, :], nm[:, s, :], bias[:, 1, :], ALU.mult).then_inc(psem("ffn", "scaled"), 1)
                dve.wait_ge(psem("ffn", "scaled"), t + 1)
                tt(nm[:, s, :], nm[:, s, :], bias[:, 2, :], ALU.add).then_inc(psem("ffn", "shifted"), 1)
                dve.wait_ge(psem("ffn", "shifted"), t + 1)
                tt(tile(acc, t, DEGW), nm[:, s, :], tile(X, t), ALU.add).then_inc(psem("ffn", "v"), 1)
                row_stats("ffn", t, s)
            over_tiles(dve, ffn_tile)
            barrier(dve, 20)
            layer_norm("ln3", 9)
            barrier(dve, 21)


_INS = ["x", "src", "dst", "edge_attr_256", "edge_weight",
        "L0_gnn_w1", "L0_gnn_b1", "L0_gnn_g1", "L0_gnn_beta1", "L0_gnn_wr", "L0_gnn_br", "L0_gnn_wroot",
        "L0_gnn_w2", "L0_gnn_b2", "L0_gnn_g2", "L0_gnn_beta2", "L1_gnn_W", "L1_gnn_b",
        "L2_gnn_W1", "L2_gnn_b1", "L2_gnn_W2", "L2_gnn_b2", "L2_gnn_W3", "L2_gnn_b3",
        "L3_gnn_W1", "L3_gnn_b1", "L3_gnn_W2", "L3_gnn_b2",
        "L3_gnn_bn1_gamma", "L3_gnn_bn1_beta", "L3_gnn_bn1_mean", "L3_gnn_bn1_var",
        "L3_gnn_bn2_gamma", "L3_gnn_bn2_beta", "L3_gnn_bn2_mean", "L3_gnn_bn2_var"]


def kernel(**inputs):
    import numpy as _np
    import concourse.bacc as _bacc
    from concourse import mybir as _mybir
    from concourse.bass_utils import run_bass_kernel_spmd as _run

    nc = _bacc.Bacc("TRN2", target_bir_lowering=False, num_devices=1)
    arrays, args = {}, {}
    for name in _INS:
        arr = _np.ascontiguousarray(inputs[name])
        arrays[f"in_{name}_dram"] = arr
        args[name] = nc.dram_tensor(f"in_{name}_dram", arr.shape, _mybir.dt.from_np(arr.dtype), kind="ExternalInput").ap()
    n, d = inputs["x"].shape
    out = nc.dram_tensor("out_0_dram", (n, d), _mybir.dt.float32, kind="ExternalOutput").ap()
    gnn_kernel(nc, args, out)
    r = _run(nc, [arrays], core_ids=[0])
    return r.results[0]["out_0_dram"]
```

```python
from contextlib import ExitStack

import concourse.bass as bass
from concourse import mybir

P = 128
ALU = mybir.AluOpType
ACT = mybir.ActivationFunctionType
F32 = mybir.dt.float32
I32 = mybir.dt.int32
BF16 = mybir.dt.bfloat16
EPS = 1e-5
ds = bass.ds

RING = 16
BATCH = 4
ONEHOTS = 8
MSGS = 4
MSG_LEAD = 2
SUMS = 4
PARTS = 3
REC = 3


def gnn_kernel(nc, a, out):
    N, D = a["x"].shape
    E = a["src"].shape[0]
    T = -(-N // P)
    LAST = N - (T - 1) * P
    NP = T * P
    C = -(-(E + T * (P - 1)) // (P * RING)) * RING
    FE = -(-E // (P * RING)) * RING
    PFULL = E // FE
    REST = E - PFULL * FE
    DH = D // P
    DEGW = D + 1
    RINGW = PARTS * D // 2 + 1
    NO_TILE = P * (T + 1)
    assert DH == 2 and PFULL == P - 1 and REST > 0 and T % 2 == 1 and T < 64

    rec_dram = {k: nc.dram_tensor(f"records_by_{k}", (P * C + FE, REC), F32).ap() for k in ("dst", "src")}
    tiles_dram = {k: nc.dram_tensor(f"tile_of_chunk_by_{k}", (1, C), I32).ap() for k in ("dst", "src")}
    table = {k: nc.dram_tensor(f"table_{k}", (NP, D), F32).ap() for k in ("x1", "x3")}
    table |= {k: nc.dram_tensor(f"table_{k}", (NP, PARTS * D), BF16).ap() for k in ("h", "g0", "g1", "g2")}

    with ExitStack() as ctx:
        def sb(name, shape, dt=F32):
            return ctx.enter_context(nc.sbuf_tensor(name, shape, dt))

        def sem(name):
            return ctx.enter_context(nc.semaphore(name))

        bank = [ctx.enter_context(nc.psum_tensor(f"bank{i}", [P, 512], F32)) for i in range(8)]

        X = sb("X", [P, T * D])
        H = sb("H", [P, T * D])
        acc = sb("acc", [P, T * DEGW])
        rec = sb("rec", [P, C * REC])
        tile_row = sb("tile_row", [1, C], I32)
        ring_mem = sb("ring_mem", [P, RING * RINGW])
        idx_ring = sb("idx_ring", [P, RING], I32)
        eid_ring = sb("eid_ring", [P, RING], I32)
        onehot = sb("onehot", [P, ONEHOTS, P])
        onehot_bf = onehot[:, :, :].rearrange("p s j -> p (s j)").bitcast(BF16)\
            .rearrange("p (s j) -> p s j", s=ONEHOTS)[:, :, 0:P]
        rec_v = rec[:, :].rearrange("p (c w) -> p c w", w=REC)
        G = ring_mem[:, 0:RING * D].rearrange("p (s d) -> p s d", s=RING)
        GP = ring_mem[:, :].bitcast(BF16).rearrange("p (s d) -> p s d", s=RING)
        EA = H[:, 0:RING * D].rearrange("p (s d) -> p s d", s=RING)
        M = H[:, RING * D:(RING + MSGS) * D].rearrange("p (s d) -> p s d", s=MSGS)

        iota_row = sb("iota_row", [P, P])
        iota_bf = sb("iota_bf", [P, P], BF16)
        ident = sb("ident", [P, P])
        below = sb("below", [P, P])
        upto = sb("upto", [P, P])
        ones = sb("ones", [P, P])

        wt = {k: sb(f"wt_{k}", [P, DH, D]) for k in ("a", "b", "c", "d")}
        pcol = sb("pcol", [P, 9, DH])
        bias = sb("bias", [P, 4, D])
        stats = sb("stats", [P, DH, T * 6])
        ln_stats = stats[:, 0, :]
        ln_w = sb("ln_w", [P, 3, T])
        mean = sb("mean", [P, T])
        std = sb("std", [P, T])
        rstd = sb("rstd", [P, T])
        dis_r = sb("dis_r", [P, T])
        dis = sb("dis", [P, T])
        bn_mv = sb("bn_mv", [P, DH, 2])
        bn_s = sb("bn_s", [P, 4, DH])

        def stage(i):
            return ring_mem[:, 2 * i * D:2 * (i + 1) * D].rearrange("p (s d) -> p s d", s=2)

        stg, fT, hT, gT, nm, rest = (stage(i) for i in range(6))
        parts = ring_mem[:, 12 * D:12 * D + PARTS * D].bitcast(BF16).rearrange("p (s q d) -> p s q d", s=2, q=PARTS)

        cnt = ring_mem[:, 16 * D:16 * D + 6 * 64].rearrange("p (w t) -> p w t", w=6)
        cnt_i = ring_mem[:, 18 * D:18 * D + 2 * 64].bitcast(I32).rearrange("p (w t) -> p w t", w=2)

        def acc_cols(i, n=1, dt=F32):
            part = acc[:, i * FE:(i + n) * FE]
            return part if dt == F32 else part.bitcast(dt)

        ends = {"dst": acc_cols(0, 1, I32), "src": acc_cols(1, 1, I32)}
        weight = acc_cols(2)
        key = acc_cols(3)
        scan = acc_cols(4)
        mask = acc_cols(5)
        tmp_i = acc_cols(6, 1, I32)
        slot_f = acc_cols(7)
        slot_i = {"dst": acc_cols(8, 1, I32), "src": acc_cols(9, 1, I32)}
        rec_e = acc_cols(10, REC)
        chunk_no = rec[:, 0:C]
        chunk_cmp = rec[:, C:2 * C]
        edge_no = rec_e.rearrange("p (f w) -> p f w", w=REC)[:, :, 2]
        rec_ev = rec_e.rearrange("p (f w) -> p f w", w=REC)
        scan_i = scan.bitcast(I32)
        mask_i = mask.bitcast(I32)
        idx_stage = idx_ring
        rec_stage = sb("rec_stage", [P, RING, REC])
        rec_stage_flat = rec_stage[:, :, :].rearrange("p s w -> p (s w)")
        assert (10 + REC) * FE <= T * DEGW
        wnat = H[:, 0:4 * DH * D].rearrange("p (q h d) -> p q h d", q=4, h=DH)

        phase_end = sem("phase_end")
        spaced = sem("spaced")
        gathered = [sem(f"gathered{i}") for i in range(RING)]
        ea_in = [sem(f"ea_in{i}") for i in range(RING)]
        scattered = [sem(f"scattered{i}") for i in range(RING // BATCH)]
        staged = sem("staged")
        idx_ready = sem("idx_ready")
        summed = sem("summed")
        onehot_ready = sem("onehot_ready")
        onehot_raw = sem("onehot_raw")
        added = sem("added")
        msg_added = sem("msg_added")
        msg_relu = sem("msg_relu")
        vec_chain = sem("vec_chain")
        act_chain = sem("act_chain")
        pool_chain = sem("pool_chain")
        loads = sem("loads")
        edges_in = sem("edges_in")
        stores = sem("stores")
        fills = sem("fills")
        sorts = sem("sorts")
        counts = sem("counts")
        w_in = sem("w_in")
        w_turned = sem("w_turned")
        w_copied = sem("w_copied")
        ln_var = sem("ln_var")
        ln_std = sem("ln_std")
        vars_in = sem("vars_in")

        made = {}

        def psem(phase, what):
            name = "gcn" if phase in ("gcn0", "gcn1") else phase
            if (name, what) not in made:
                made[name, what] = sem(f"{name}_{what}")
            return made[name, what]

        def after(phase, what, n):
            each = {"written0": 16 * (T // 2 + 1), "written1": 16 * (T // 2)}.get(what, T)
            return psem(phase, what), n + (each if phase == "gcn1" else 0)

        block = ctx.enter_context(nc.Block())

        def barrier(eng, k):
            eng.drain().then_inc(phase_end, 1)
            eng.wait_ge(phase_end, 5 * k)

        def hold(eng, sm, value):
            eng.wait_ge(sm, value)
            if not isinstance(value, int):
                eng.sem_inc(spaced, 1)

        def over_tiles(eng, *stages):
            stages = [st if isinstance(st, tuple) else (st, 0) for st in stages]
            most = max(lag for _, lag in stages)
            first = (most + 3) // 2 * 2

            def step(t, parity):
                for f, lag in stages:
                    if not isinstance(t, int) or 0 <= t - lag < T:
                        f(t - lag, (parity - lag) % 2, not isinstance(t, int) or t - lag >= 2)

            for t in range(first):
                step(t, t % 2)
            with eng.Fori(0, (T - 1 - first) // 2) as i:
                step(i * 2 + first, 0)
                step(i * 2 + (first + 1), 1)
            for t in range(T - 1, T + most):
                step(t, t % 2)

        def tile(buf, t, width=D, cols=D):
            return buf[:, ds(t * width, cols)]

        AGGS = [("dst", "h", False, True, False), ("src", "x1", True, False, False),
                ("dst", "g0", False, False, False), ("dst", "g1", False, False, False),
                ("dst", "g2", False, False, False), ("dst", "x3", False, False, True)]

        @block.sync
        def _(sp):
            total = {"loads": 0, "stores": 0}

            def load(dst, src, sm=loads, name="loads"):
                sp.dma_start(dst, src).then_inc(sm, 16)
                if name in total:
                    total[name] += 16

            def loaded():
                sp.wait_ge(loads, total["loads"])

            def store(dst, src):
                sp.dma_start(dst, src).then_inc(stores, 16)
                total["stores"] += 16

            def columns(i, name):
                with nc.allow_non_contiguous_dma(reason="256 words"):
                    load(pcol[:, i, :], a[name].rearrange("(h p) -> p h", p=P))

            def bias_row(i, name):
                load(bias[:, i, :], a[name].rearrange("(o d) -> o d", o=1).to_broadcast((P, D)))

            def weights(k, name):
                load(wt[k][:, :, :], a[name].rearrange("(h k) n -> k h n", k=P))

            def natural_weights(names):
                for q, name in enumerate(names):
                    sp.dma_start(wnat[:, q, :, :], a[name].rearrange("(h o) k -> o h k", o=P)).then_inc(w_in, 16)

            def write_table(phase, buf, name):
                def body(t, s, used):
                    sp.wait_ge(*after(phase, "rows", t + 1))
                    sp.dma_start(table[name][ds(t * P, P), :], tile(buf, t)).then_inc(psem(phase, "written"), 16)
                over_tiles(sp, body)
                sp.wait_ge(*after(phase, "written", 16 * T))

            def write_parts(phase, name):
                def body(t, s, used):
                    sp.wait_ge(*after(phase, "parts", t + 1))
                    sp.dma_start(table[name][ds(t * P, P), :], parts[:, s, :, :].rearrange("p q d -> p (q d)"))\
                      .then_inc(psem(phase, f"written{s}"), 16)
                over_tiles(sp, body)
                sp.wait_ge(*after(phase, "written0", 16 * (T // 2 + 1)))
                sp.wait_ge(*after(phase, "written1", 16 * (T // 2)))

            def load_records(which):
                load(rec[:, :], rec_dram[which][0:P * C, :].rearrange("(p c) w -> p (c w)", p=P))
                load(tile_row[:, :], tiles_dram[which])
                loaded()

            sp.wait_ge(fills, 1)
            for k in ("dst", "src"):
                sp.dma_start(ends[k][0:PFULL, :], a[k][0:PFULL * FE].rearrange("(p f) -> p f", p=PFULL)).then_inc(edges_in, 16)
                sp.dma_start(ends[k][PFULL:P, 0:REST], a[k][PFULL * FE:E].rearrange("(p f) -> p f", p=1)).then_inc(edges_in, 16)
            sp.dma_start(weight[0:PFULL, :], a["edge_weight"][0:PFULL * FE].rearrange("(p f) -> p f", p=PFULL)).then_inc(edges_in, 16)
            sp.dma_start(weight[PFULL:P, 0:REST], a["edge_weight"][PFULL * FE:E].rearrange("(p f) -> p f", p=1)).then_inc(edges_in, 16)
            natural_weights(("L0_gnn_w1", "L0_gnn_wr", "L0_gnn_wroot", "L0_gnn_w2"))
            for i, name in enumerate(("b1", "g1", "beta1", "br", "b2", "g2", "beta2")):
                columns(i, "L0_gnn_" + name)
            load(X[:, 0:(T - 1) * D].rearrange("p (t d) -> p t d", d=D),
                 a["x"][0:(T - 1) * P, :].rearrange("(t p) d -> p t d", p=P))
            load(X[0:LAST, (T - 1) * D:T * D], a["x"][(T - 1) * P:N, :])
            sp.wait_ge(fills, 2)
            for k in ("dst", "src"):
                store(rec_dram[k][0:P * C, :].rearrange("(p c) w -> p (c w)", p=P), rec[:, :])
            sp.wait_ge(stores, total["stores"])
            sp.sem_inc(psem("sort", "padded"), 1)
            sp.wait_ge(psem("sort", "tiles"), 1)
            store(tiles_dram["dst"], tile_row[:, :])
            sp.wait_ge(stores, total["stores"])
            loaded()
            barrier(sp, 1)
            write_parts("h", "h")
            sp.wait_ge(psem("sort", "tiles"), 2)
            store(tiles_dram["src"], tile_row[:, :])
            sp.wait_ge(stores, total["stores"])
            barrier(sp, 2)
            barrier(sp, 3)
            load_records("dst")
            barrier(sp, 4)
            barrier(sp, 5)
            barrier(sp, 6)
            load_records("src")
            weights("a", "L1_gnn_W")
            bias_row(0, "L1_gnn_b")
            loaded()
            write_table("ln0", X, "x1")
            barrier(sp, 7)
            barrier(sp, 8)
            load_records("dst")
            barrier(sp, 9)
            weights("a", "L2_gnn_W1")
            weights("b", "L2_gnn_W2")
            weights("c", "L2_gnn_W3")
            for i in range(3):
                bias_row(i, f"L2_gnn_b{i + 1}")
            loaded()
            write_parts("ln1", "g0")
            barrier(sp, 10)
            barrier(sp, 11)
            write_parts("gcn0", "g1")
            barrier(sp, 12)
            barrier(sp, 13)
            write_parts("gcn1", "g2")
            barrier(sp, 14)
            barrier(sp, 15)
            barrier(sp, 16)
            natural_weights(("L3_gnn_W1", "L3_gnn_W2"))
            bias_row(0, "L3_gnn_b2")
            for i, name in enumerate(("b1", "bn1_gamma", "bn1_beta", "bn1_mean", "bn1_var")):
                columns(i, "L3_gnn_" + name)
            loaded()
            write_table("ln2", X, "x3")
            barrier(sp, 17)
            barrier(sp, 18)
            for i, name in enumerate(("gamma", "beta", "mean", "var")):
                sp.dma_start(H[:, i * D:(i + 1) * D], a["L3_gnn_bn2_" + name].rearrange("(o d) -> o d", o=1)
                             .to_broadcast((P, D))).then_inc(psem("norm2", "in"), 16)
            sp.wait_ge(psem("norm2", "in"), 64)
            barrier(sp, 19)
            barrier(sp, 20)

            def out_rows(t, s, used):
                sp.wait_ge(psem("ln3", "rows"), t + 1)
                if isinstance(t, int) and t == T - 1:
                    sp.dma_start(out[t * P:N, :], X[0:LAST, t * D:(t + 1) * D]).then_inc(psem("ln3", "written"), 16)
                else:
                    sp.dma_start(out[ds(t * P, P), :], tile(X, t)).then_inc(psem("ln3", "written"), 16)
            over_tiles(sp, out_rows)
            sp.wait_ge(psem("ln3", "written"), 16 * T)
            barrier(sp, 21)

        @block.gpsimd
        def _(pool):
            chain = [0]

            def link(ins):
                chain[0] += 1
                ins.then_inc(pool_chain, 1)
                pool.wait_ge(pool_chain, chain[0])

            nc.gpsimd.iota(iota_row[:, :], [[1, P]], 0, channel_multiplier=0, allow_small_or_imprecise_dtypes=True)
            nc.gpsimd.memset(ones[:, :], 1.0)
            link(nc.gpsimd.memset(ident[:, :], 0.0))
            nc.gpsimd.affine_select(out=ident[:, :], in_=ident[:, :], compare_op=ALU.not_equal, fill=1.0,
                                    base=0, pattern=[[-1, P]], channel_multiplier=1).then_inc(counts, 1)
            pool.wait_ge(pool_chain, 1)
            link(nc.gpsimd.affine_select(out=below[:, :], in_=ones[:, :], compare_op=ALU.is_gt, fill=0.0,
                                         base=0, pattern=[[1, P]], channel_multiplier=-1))
            link(nc.gpsimd.affine_select(out=upto[:, :], in_=ones[:, :], compare_op=ALU.is_ge, fill=0.0,
                                         base=0, pattern=[[1, P]], channel_multiplier=-1))
            link(nc.gpsimd.iota(edge_no, [[1, FE]], 0, channel_multiplier=FE, allow_small_or_imprecise_dtypes=True))
            pool.sem_inc(counts, 1)

            def scatter(k):
                which = ("dst", "src")[k]
                base = 4 * 16 * (FE // RING) * k

                def body(i):
                    for g in range(RING // BATCH):
                        at = i * RING + g * BATCH
                        if not (isinstance(i, int) and i == 0):
                            hold(pool, scattered[g], i * (16 * BATCH) + base)
                        nc.gpsimd.tensor_copy(idx_stage[:, g * BATCH:(g + 1) * BATCH], slot_i[which][:, ds(at, BATCH)])
                        nc.gpsimd.tensor_copy(rec_stage_flat[:, g * BATCH * REC:(g + 1) * BATCH * REC],
                                              rec_e[:, ds(at * REC, BATCH * REC)]).then_inc(staged, 1)
                        hold(pool, staged, i * (RING // BATCH) + g + 1 + k * (FE // BATCH))
                        for j in range(g * BATCH, (g + 1) * BATCH):
                            pool.indirect_dma_start(
                                out=rec_dram[which][:, :], out_offset=bass.IndirectOffsetOnAxis(ap=idx_stage[:, j:j + 1], axis=0),
                                in_=rec_stage[:, j, :], in_offset=None).then_inc(scattered[g], 16)
                body(0)
                with pool.Fori(1, FE // RING) as i:
                    body(i)
                for g in range(RING // BATCH):
                    pool.wait_ge(scattered[g], base + 16 * BATCH * (FE // RING))

            def third_parts(phase):
                def body(t, s, used):
                    hold(pool, *after(phase, "second", t + 1))
                    nc.gpsimd.tensor_tensor(parts[:, s, 2, :], rest[:, s, :], parts[:, s, 1, :], ALU.subtract)\
                      .then_inc(psem(phase, "parts"), 1)
                over_tiles(pool, body)

            def gather(n):
                which, name, weighted, counted, edges = AGGS[n]
                rows = G if weighted or edges else GP[:, :, 0:PARTS * D]
                with pool.Fori(0, C // RING) as i:
                    for s in range(RING):
                        if s % BATCH == 0:
                            hold(pool, idx_ready, i * (RING // BATCH) + s // BATCH + 1 + n * (C // BATCH))
                        pool.indirect_dma_start(
                            out=rows[:, s, :], out_offset=None, in_=table[name][:, :],
                            in_offset=bass.IndirectOffsetOnAxis(ap=idx_ring[:, s:s + 1], axis=0)).then_inc(gathered[s], 16)
                        if edges:
                            pool.indirect_dma_start(
                                out=EA[:, s, :], out_offset=None, in_=a["edge_attr_256"][:, :],
                                in_offset=bass.IndirectOffsetOnAxis(ap=eid_ring[:, s:s + 1], axis=0)).then_inc(ea_in[s], 16)

            pool.wait_ge(psem("sort", "padded"), 1)
            nc.gpsimd.iota(chunk_no, [[1, C]], 0, channel_multiplier=0,
                           allow_small_or_imprecise_dtypes=True).then_inc(psem("sort", "chunk_no"), 1)
            barrier(pool, 1)
            scatter(0)
            barrier(pool, 2)
            barrier(pool, 3)
            scatter(1)
            barrier(pool, 4)
            gather(0)
            barrier(pool, 5)
            barrier(pool, 6)
            barrier(pool, 7)
            gather(1)
            barrier(pool, 8)
            barrier(pool, 9)
            third_parts("ln1")
            barrier(pool, 10)
            gather(2)
            barrier(pool, 11)
            third_parts("gcn0")
            barrier(pool, 12)
            gather(3)
            barrier(pool, 13)
            third_parts("gcn1")
            barrier(pool, 14)
            gather(4)
            barrier(pool, 15)
            barrier(pool, 16)
            barrier(pool, 17)
            gather(5)
            for k in range(18, 22):
                barrier(pool, k)

        @block.tensor
        def _(pe):
            def sum_chunks(n):
                which, name, weighted, counted, edges = AGGS[n]
                with pe.Fori(0, C // RING) as i:
                    for s in range(RING):
                        c = i * RING + s + n * C
                        sum_ = bank[s % SUMS]
                        if s % BATCH == 0:
                            pe.wait_ge(onehot_ready, i * (RING // BATCH) + s // BATCH + 1 + n * (C // BATCH))
                        if edges:
                            pe.wait_ge(msg_relu, i * RING + s + 1)
                        else:
                            pe.wait_ge(gathered[s], i * 16 + 16 + n * 16 * (C // RING))
                        pe.wait_ge(added, c + (RING + 2 - SUMS))
                        if weighted or edges:
                            rows = M[:, s % MSGS, :] if edges else G[:, s, :]
                            last = pe.matmul(sum_[:, 0:D], onehot[:, s % ONEHOTS, :], rows, start=True, stop=True)
                        else:
                            for q in reversed(range(PARTS)):
                                width = DEGW if counted and q == PARTS - 1 else D
                                last = pe.matmul(sum_[:, 0:width], onehot_bf[:, s % ONEHOTS, :],
                                                 GP[:, s, q * D:q * D + width], start=(q == PARTS - 1), stop=(q == 0),
                                                 skip_group_check=True)
                        last.then_inc(summed, 1)

            def turn(phase, src, to, s):
                for h in range(DH):
                    last = pe.transpose(to[:, h * P:(h + 1) * P], src[:, s, h * P:(h + 1) * P], ident[:, :])
                last.then_inc(psem(phase, "turned"), 1)

            def to_features(dst, pairs):
                for o in range(DH):
                    n = 0
                    for wk, val in pairs:
                        for k in range(DH):
                            last = pe.matmul(dst[:, o * P:(o + 1) * P], wk[:, k, o * P:(o + 1) * P],
                                             val[:, k * P:(k + 1) * P], start=(n == 0), stop=(n == DH * len(pairs) - 1))
                            n += 1
                return last

            def to_nodes(dst, wk, val, row=None):
                for k in range(DH):
                    last = pe.matmul(dst[:, 0:D], val[:, k * P:(k + 1) * P], wk[:, k, :], start=(k == 0),
                                     stop=(k == DH - 1 and row is None))
                if row is not None:
                    last = pe.matmul(dst[:, 0:D], ones[0:1, :], row, start=False, stop=True)
                return last

            def sort_counts(k):
                pe.wait_ge(sorts, 3 * k + 1)
                pe.matmul(bank[0][:, 0:T], below[:, :], cnt[:, 0, 0:T], start=True, stop=True)
                pe.matmul(bank[1][:, 0:T], ones[:, :], cnt[:, 0, 0:T], start=True, stop=True)
                pe.matmul(bank[2][0:T, 0:1], cnt[:, 0, 0:T], ones[:, 0:1], start=True, stop=True).then_inc(psem("sort", "mm"), 1)
                pe.wait_ge(sorts, 3 * k + 2)
                pe.matmul(bank[3][0:T, 0:1], upto[0:T, 0:T], cnt[0:T, 5, 0:1], start=True, stop=True).then_inc(psem("sort", "mm"), 1)
                pe.wait_ge(sorts, 3 * k + 3)
                pe.matmul(bank[0][0:1, 0:512], ones[0:T, 0:1], chunk_cmp[0:T, 0:512], start=True, stop=True)
                pe.matmul(bank[1][0:1, 0:C - 512], ones[0:T, 0:1], chunk_cmp[0:T, 512:C], start=True, stop=True).then_inc(psem("sort", "mm"), 1)

            def turn_weights(n, before):
                pe.wait_ge(w_in, 16 * (before + n))
                for q in range(n):
                    if q >= 2:
                        pe.wait_ge(w_copied, before + q - 1)
                    for k in range(DH):
                        for o in range(DH):
                            last = pe.transpose(bank[4 + q % 2][:, k * D + o * P:k * D + (o + 1) * P],
                                                wnat[:, q, o, k * P:(k + 1) * P], ident[:, :])
                    last.then_inc(w_turned, 1)

            pe.wait_ge(counts, 2)
            turn_weights(4, 0)
            sort_counts(0)
            barrier(pe, 1)

            def turn_staged(phase, src, first_bank, ready, free):
                def body(t, s, used):
                    pe.wait_ge(*after(phase, ready, t + 1))
                    if used:
                        pe.wait_ge(*after(phase, free, t - 1))
                    turn(phase, src, bank[first_bank + s], s)
                return body

            def y_product(t, s, used):
                pe.wait_ge(psem("y", "fT"), t + 1)
                if used:
                    pe.wait_ge(psem("y", "kept"), t - 1)
                to_features(bank[6 + s], [(wt["a"], fT[:, s, :])]).then_inc(psem("y", "product"), 1)
            over_tiles(pe, (turn_staged("y", stg, 4, "staged", "fT"), 0), (y_product, 1))
            over_tiles(pe, turn_staged("h", hT, 2, "scaled", "rows"))
            sort_counts(1)
            barrier(pe, 2)
            barrier(pe, 3)
            barrier(pe, 4)
            sum_chunks(0)
            barrier(pe, 5)

            def conv_mid(t, s, used):
                pe.wait_ge(psem("conv", "hT"), t + 1)
                pe.wait_ge(psem("conv", "fT"), t + 1)
                if used:
                    pe.wait_ge(psem("conv", "gT"), t - 1)
                to_features(bank[2 + s], [(wt["b"], fT[:, s, :]), (wt["c"], hT[:, s, :])]).then_inc(psem("conv", "mid"), 1)

            def conv_product(t, s, used):
                pe.wait_ge(psem("conv", "gT"), t + 1)
                if used:
                    pe.wait_ge(psem("conv", "kept"), t - 1)
                to_features(bank[4 + s], [(wt["d"], gT[:, s, :])]).then_inc(psem("conv", "product"), 1)
            over_tiles(pe, (turn_staged("conv", stg, 0, "staged", "fT"), 0), (conv_mid, 1), (conv_product, 2))
            over_tiles(pe, turn_staged("z", hT, 6, "scaled", "v"))
            barrier(pe, 6)
            barrier(pe, 7)
            sum_chunks(1)
            barrier(pe, 8)

            def linear(phase, wk, row, taken="taken"):
                def product(t, s, used):
                    pe.wait_ge(*after(phase, "fT", t + 1))
                    if used:
                        pe.wait_ge(*after(phase, taken, t - 1))
                    to_nodes(bank[2 + s], wk, fT[:, s, :], row).then_inc(psem(phase, "product"), 1)
                over_tiles(pe, (turn_staged(phase, stg, 0, "staged", "fT"), 0), (product, 1))

            linear("lin1", wt["a"], bias[0:1, 0, :], "v")
            barrier(pe, 9)
            barrier(pe, 10)
            sum_chunks(2)
            barrier(pe, 11)
            linear("gcn0", wt["a"], None)
            barrier(pe, 12)
            sum_chunks(3)
            barrier(pe, 13)
            linear("gcn1", wt["b"], None)
            barrier(pe, 14)
            sum_chunks(4)
            barrier(pe, 15)
            linear("gcn2", wt["c"], None)
            barrier(pe, 16)
            turn_weights(2, 4)
            barrier(pe, 17)
            sum_chunks(5)
            barrier(pe, 18)
            barrier(pe, 19)

            def ffn_mid(t, s, used):
                pe.wait_ge(psem("ffn", "fT"), t + 1)
                if used:
                    pe.wait_ge(psem("ffn", "gT"), t - 1)
                to_features(bank[2 + s], [(wt["a"], fT[:, s, :])]).then_inc(psem("ffn", "mid"), 1)

            def ffn_product(t, s, used):
                pe.wait_ge(psem("ffn", "gT"), t + 1)
                if used:
                    pe.wait_ge(psem("ffn", "taken"), t - 1)
                to_nodes(bank[4 + s], wt["b"], gT[:, s, :], bias[0:1, 0, :]).then_inc(psem("ffn", "product"), 1)
            over_tiles(pe, (turn_staged("ffn", stg, 0, "staged", "fT"), 0), (ffn_mid, 1), (ffn_product, 2))
            barrier(pe, 20)
            barrier(pe, 21)

        @block.scalar
        def _(act):
            def copy_turned(phase, s, t, used, reader, src, scale=None, shift=None):
                act.wait_ge(*after(phase, "turned", t + 1))
                if used:
                    hold(act, *after(phase, reader, t - 1))
                if scale is None:
                    nc.scalar.copy(fT[:, s, :], src[:, 0:D]).then_inc(psem(phase, "fT"), 1)
                else:
                    for h in range(DH):
                        last = nc.scalar.activation(fT[:, s, h * P:(h + 1) * P], src[:, h * P:(h + 1) * P], ACT.Identity,
                                                    bias=shift[:, h:h + 1], scale=scale[:, h:h + 1])
                    last.then_inc(psem(phase, "fT"), 1)

            def normed(phase, t, s, used, reader, what):
                if used:
                    hold(act, *after(phase, reader, t - 1))
                for h in range(DH):
                    last = nc.scalar.activation(hT[:, s, h * P:(h + 1) * P], H[:, ds(t * D + h * P, P)], ACT.Identity,
                                                bias=bn_s[:, 3, h:h + 1], scale=bn_s[:, 2, h:h + 1])
                last.then_inc(psem(phase, what), 1)

            def root(out_, in_, n):
                act.wait_ge(ln_var, n)
                nc.scalar.activation(out_, in_, ACT.Sqrt).then_inc(ln_std, 1)

            def stage_indices(n):
                which, name, weighted, counted, edges = AGGS[n]

                def stage_batch(i, g):
                    at = i * RING + g * BATCH
                    hold(act, summed, at + BATCH + n * C)
                    last = nc.scalar.copy(idx_ring[:, g * BATCH:(g + 1) * BATCH], rec_v[:, ds(at, BATCH), 0])
                    if edges:
                        last = nc.scalar.copy(eid_ring[:, g * BATCH:(g + 1) * BATCH], rec_v[:, ds(at, BATCH), 2])
                    last.then_inc(idx_ready, 1)

                def relu_batch(i, g):
                    for s in range(g * BATCH, (g + 1) * BATCH):
                        act.wait_ge(msg_added, i * RING + s + 1)
                        nc.scalar.activation(M[:, s % MSGS, :], M[:, s % MSGS, :], ACT.Relu).then_inc(msg_relu, 1)

                if not edges:
                    with act.Fori(0, C // RING) as i:
                        for g in range(RING // BATCH):
                            stage_batch(i, g)
                    return
                for g in range(RING // BATCH - 1):
                    stage_batch(0, g)
                with act.Fori(0, C // RING - 1) as i:
                    for g in range(RING // BATCH):
                        ahead = g + RING // BATCH - 1
                        stage_batch(i + ahead // (RING // BATCH), ahead % (RING // BATCH))
                        relu_batch(i, g)
                i = C // RING - 1
                stage_batch(i, RING // BATCH - 1)
                for g in range(RING // BATCH):
                    relu_batch(i, g)

            def copy_weights(n, before):
                for q in range(n):
                    act.wait_ge(w_turned, before + q + 1)
                    nc.scalar.copy(wt["abcd"[q]][:, :, :].rearrange("p h d -> p (h d)"), bank[4 + q % 2][:, :])\
                      .then_inc(w_copied, 1)

            copy_weights(4, 0)
            barrier(act, 1)

            def split_parts(phase, src):
                def first(t, s, used):
                    act.wait_ge(*after(phase, "rows", t + 1))
                    if used:
                        hold(act, *after(phase, f"written{s}", (t - s) * 8))
                    nc.scalar.copy(parts[:, s, 0, :], src(t, s)).then_inc(psem(phase, "first"), 1)

                def second(t, s, used):
                    act.wait_ge(*after(phase, "left", t + 1))
                    nc.scalar.copy(parts[:, s, 1, :], rest[:, s, :]).then_inc(psem(phase, "second"), 1)
                return first, second

            def y_keep(t, s, used):
                hold(act, psem("y", "product"), t + 1)
                for h in range(DH):
                    last = nc.scalar.activation(H[:, ds(t * D + h * P, P)], bank[6 + s][:, h * P:(h + 1) * P],
                                                ACT.Identity, bias=pcol[:, 0, h:h + 1])
                last.then_inc(psem("y", "kept"), 1)
            over_tiles(act, (lambda t, s, used: copy_turned("y", s, t, used, "product", bank[4 + s]), 0), (y_keep, 1))
            root(bn_s[:, 1, :], bn_s[:, 0, :], 1)
            act.wait_ge(vars_in, 1)
            first, second = split_parts("h", lambda t, s: nm[:, s, :])
            over_tiles(act, (lambda t, s, used: normed("h", t, s, used, "turned", "scaled"), 0), (first, 1), (second, 2))
            barrier(act, 2)
            barrier(act, 3)
            barrier(act, 4)
            stage_indices(0)
            barrier(act, 5)

            def conv_in(t, s, used):
                copy_turned("conv", s, t, used, "mid", bank[0 + s])
                normed("conv", t, s, used, "mid", "hT")

            def conv_gelu(t, s, used):
                act.wait_ge(psem("conv", "mid"), t + 1)
                if used:
                    hold(act, psem("conv", "product"), t - 1)
                for h in range(DH):
                    last = nc.scalar.activation(gT[:, s, h * P:(h + 1) * P], bank[2 + s][:, h * P:(h + 1) * P],
                                                ACT.Gelu, bias=pcol[:, 3, h:h + 1])
                last.then_inc(psem("conv", "gT"), 1)
            over_tiles(act, (conv_in, 0), (conv_gelu, 1))
            root(bn_s[:, 1, :], bn_s[:, 0, :], 2)
            act.wait_ge(vars_in, 2)
            over_tiles(act, lambda t, s, used: normed("z", t, s, used, "turned", "scaled"))
            barrier(act, 6)
            root(std[:, :], rstd[:, :], 3)
            root(dis[:, :], dis_r[:, :], 4)
            barrier(act, 7)
            stage_indices(1)
            barrier(act, 8)
            over_tiles(act, lambda t, s, used: copy_turned("lin1", s, t, used, "product", bank[0 + s]))
            barrier(act, 9)
            root(std[:, :], rstd[:, :], 5)
            first, second = split_parts("ln1", lambda t, s: tile(H, t))
            over_tiles(act, (first, 0), (second, 1))
            barrier(act, 10)
            stage_indices(2)
            barrier(act, 11)

            def gcn_stages(phase):
                def gelu(t, s, used):
                    act.wait_ge(*after(phase, "taken", t + 1))
                    if used:
                        hold(act, *after(phase, "rows", t - 1))
                    nc.scalar.activation(hT[:, s, :], gT[:, s, :], ACT.Gelu_apprx_tanh).then_inc(psem(phase, "gelu"), 1)
                first, second = split_parts(phase, lambda t, s: tile(H, t))
                return ((lambda t, s, used: copy_turned(phase, s, t, used, "product", bank[0 + s]), 0), (gelu, 2),
                        (first, 3), (second, 4))
            over_tiles(act, *gcn_stages("gcn0"))
            barrier(act, 12)
            stage_indices(3)
            barrier(act, 13)
            over_tiles(act, *gcn_stages("gcn1"))
            barrier(act, 14)
            stage_indices(4)
            barrier(act, 15)
            over_tiles(act, lambda t, s, used: copy_turned("gcn2", s, t, used, "product", bank[0 + s]))
            barrier(act, 16)
            root(std[:, :], rstd[:, :], 6)
            copy_weights(2, 4)
            barrier(act, 17)
            stage_indices(5)
            barrier(act, 18)
            root(bn_s[:, 1, :], bn_s[:, 0, :], 7)
            root(bias[:, 3, :], H[:, 3 * D:4 * D], 8)
            barrier(act, 19)

            def ffn_gelu(t, s, used):
                act.wait_ge(psem("ffn", "mid"), t + 1)
                if used:
                    hold(act, psem("ffn", "product"), t - 1)
                for h in range(DH):
                    last = nc.scalar.activation(gT[:, s, h * P:(h + 1) * P], bank[2 + s][:, h * P:(h + 1) * P],
                                                ACT.Gelu, bias=pcol[:, 0, h:h + 1])
                last.then_inc(psem("ffn", "gT"), 1)
            over_tiles(act, (lambda t, s, used: copy_turned("ffn", s, t, used, "mid", bank[0 + s], bn_s[:, 2, :],
                                                            bn_s[:, 3, :]), 0), (ffn_gelu, 1))
            barrier(act, 20)
            root(std[:, :], rstd[:, :], 9)
            barrier(act, 21)

        @block.vector
        def _(dve):
            chain = [0]
            ts, tt, stt = nc.vector.tensor_scalar, nc.vector.tensor_tensor, nc.vector.scalar_tensor_tensor

            def link(ins):
                chain[0] += 1
                ins.then_inc(vec_chain, 1)
                dve.wait_ge(vec_chain, chain[0])

            def sort(k):
                own, other = (("dst", "src"), ("src", "dst"))[k]
                link(ts(tmp_i, ends[own], 7, None, ALU.logical_shift_right))
                link(nc.vector.tensor_copy(key, tmp_i))
                base = chain[0]
                with dve.Fori(0, T) as b:
                    nc.vector.tensor_scalar(mask, key, iota_row[:, ds(b, 1)], 0.0, ALU.is_equal, ALU.add,
                                            accum_out=cnt[:, 0, ds(b, 1)]).then_inc(vec_chain, 1)
                    hold(dve, vec_chain, b + (base + 1))
                chain[0] += T
                nc.vector.drain().then_inc(sorts, 1)
                dve.wait_ge(psem("sort", "mm"), 3 * k + 1)
                link(ts(cnt_i[:, 0, 0:T], bank[1][:, 0:T], float(P - 1), None, ALU.add))
                link(ts(cnt_i[:, 0, 0:T], cnt_i[:, 0, 0:T], 7, None, ALU.logical_shift_right))
                link(nc.vector.tensor_copy(cnt[:, 1, 0:T], cnt_i[:, 0, 0:T]))
                link(ts(cnt_i[0:T, 1, 0:1], bank[2][0:T, 0:1], float(P - 1), None, ALU.add))
                link(ts(cnt_i[0:T, 1, 0:1], cnt_i[0:T, 1, 0:1], 7, None, ALU.logical_shift_right))
                link(nc.vector.tensor_copy(cnt[0:T, 5, 0:1], cnt_i[0:T, 1, 0:1]))
                dve.sem_inc(sorts, 1)
                link(nc.vector.tensor_tensor_scan(cnt[:, 2, 0:T], cnt[:, 1, 0:T], cnt[:, 1, 0:T], 0.0, ALU.add, ALU.max))
                link(tt(cnt[:, 3, 0:T], cnt[:, 2, 0:T], cnt[:, 1, 0:T], ALU.subtract))
                link(stt(cnt[:, 4, 0:T], cnt[:, 3, 0:T], float(P), bank[0][:, 0:T], ALU.mult, ALU.add))
                dve.wait_ge(psem("sort", "mm"), 3 * k + 2)
                link(nc.vector.tensor_copy(cnt[0:T, 5, 1:2], bank[3][0:T, 0:1]))
                dve.wait_ge(psem("sort", "chunk_no"), 1)
                link(ts(chunk_cmp[0:T, :], chunk_no[0:T, :], cnt[0:T, 5, 1:2], None, ALU.is_ge))
                dve.sem_inc(sorts, 1)
                link(nc.vector.memset(slot_f, 0.0))
                base = chain[0]
                with dve.Fori(0, T) as b:
                    ts(mask, key, iota_row[:, ds(b, 1)], None, ALU.is_equal).then_inc(vec_chain, 1)
                    hold(dve, vec_chain, b * 3 + (base + 1))
                    nc.vector.tensor_tensor_scan(scan, mask, mask, cnt[:, 4, ds(b, 1)], ALU.add, ALU.max).then_inc(vec_chain, 1)
                    hold(dve, vec_chain, b * 3 + (base + 2))
                    nc.vector.copy_predicated(slot_f, mask_i, scan).then_inc(vec_chain, 1)
                    hold(dve, vec_chain, b * 3 + (base + 3))
                chain[0] += 3 * T
                link(ts(tmp_i, slot_f, -1.0, 0.0, ALU.add, ALU.max))
                link(ts(slot_f, edge_no, float(P * C - PFULL * FE), None, ALU.add))
                link(ts(scan_i, tmp_i, P - 1, None, ALU.bitwise_and))
                link(ts(tmp_i, tmp_i, 7, None, ALU.logical_shift_right))
                link(stt(scan, scan_i, float(C), tmp_i, ALU.mult, ALU.add))
                link(ts(mask, key, float(T), None, ALU.is_lt))
                link(nc.vector.copy_predicated(slot_f, mask_i, scan))
                link(nc.vector.tensor_copy(slot_i[own], slot_f))
                dve.wait_ge(psem("sort", "mm"), 3 * k + 3)
                ts(tile_row[:, 0:512], bank[0][0:1, 0:512], float(T - 1), float(DEGW), ALU.min, ALU.mult)
                link(ts(tile_row[:, 512:C], bank[1][0:1, 0:C - 512], float(T - 1), float(DEGW), ALU.min, ALU.mult))
                dve.sem_inc(psem("sort", "tiles"), 1)

            def records(k):
                own, other = (("dst", "src"), ("src", "dst"))[k]
                nc.vector.tensor_copy(rec_ev[:, :, 0], ends[other])
                link(ts(tmp_i, ends[own], P - 1, None, ALU.bitwise_and))
                link(nc.vector.tensor_copy(rec_ev[:, :, 1], tmp_i))
                if k == 1:
                    link(nc.vector.tensor_copy(rec_ev[:, :, 2], weight))

            def add_chunks(n):
                which, name, weighted, counted, edges = AGGS[n]
                width = DEGW if counted else D

                def one_hots(i, g):
                    at = i * RING + g * BATCH
                    exact = weighted or edges
                    slot = g * BATCH % ONEHOTS
                    to = (onehot if exact else onehot_bf)[:, slot:slot + BATCH, :]

                    def word(w):
                        return rec_v[:, ds(at, BATCH), w:w + 1].to_broadcast((P, BATCH, P))
                    made_ = tt(to, iota_row[:, :].unsqueeze(1).to_broadcast((P, BATCH, P)), word(1), ALU.is_equal)
                    if weighted:
                        made_.then_inc(onehot_raw, 1)
                        hold(dve, onehot_raw, i * (RING // BATCH) + g + 1)
                        made_ = tt(to, to, word(2), ALU.mult)
                    made_.then_inc(onehot_ready, 1)

                def message(i, s):
                    c = i * RING + s
                    dve.wait_ge(gathered[s], i * 16 + 16 + n * 16 * (C // RING))
                    dve.wait_ge(ea_in[s], i * 16 + 16)
                    dve.wait_ge(summed, c + n * C + (RING - MSGS + 1))
                    tt(M[:, s % MSGS, :], G[:, s, 0:D], EA[:, s, :], ALU.add).then_inc(msg_added, 1)

                def body(i, last):
                    for s in range(RING):
                        c = i * RING + s + n * C
                        column = dve.value_load(tile_row[0:1, ds(i * RING + s, 1)], min_val=0, max_val=(T - 1) * DEGW)
                        if s % BATCH == 0 and not (last and s + BATCH == RING):
                            one_hots(i + (s + BATCH) // RING, (s // BATCH + 1) % (RING // BATCH))
                        if edges and not (last and s + MSG_LEAD >= RING):
                            message(i + (s + MSG_LEAD) // RING, (s + MSG_LEAD) % RING)
                        turn_ = c + (RING + 1)
                        dve.wait_ge(summed, turn_)
                        dve.wait_ge(added, turn_)
                        to = acc[:, ds(column, width)]
                        tt(to, bank[s % SUMS][:, 0:width], to, ALU.add).then_inc(added, 1)

                one_hots(0, 0)
                if edges:
                    for s in range(MSG_LEAD):
                        message(0, s)
                with dve.Fori(0, C // RING - 1) as i:
                    body(i, False)
                body(C // RING - 1, True)

            def batch_norm(n, g, b):
                for h in range(DH):
                    link(nc.vector.bn_aggr(bn_mv[:, h, :], stats[:, h, :]))
                fixed_norm(n, bn_mv[:, :, 0], bn_mv[:, :, 1], g, b)

            def fixed_norm(n, mean, var, g, b):
                link(ts(bn_s[:, 0, :], var, EPS, None, ALU.add))
                dve.sem_inc(ln_var, 1)
                dve.wait_ge(ln_std, n)
                link(nc.vector.reciprocal(bn_s[:, 1, :], bn_s[:, 1, :]))
                link(tt(bn_s[:, 2, :], bn_s[:, 1, :], g, ALU.mult))
                link(tt(bn_s[:, 3, :], mean, bn_s[:, 2, :], ALU.mult))
                link(tt(bn_s[:, 3, :], b, bn_s[:, 3, :], ALU.subtract))

            def stage_tile(phase, src, lag=0):
                def body(t, s, used):
                    if used:
                        dve.wait_ge(*after(phase, "turned", t - 1))
                    ts(stg[:, s, :], src(t), 1.0, None, ALU.mult).then_inc(psem(phase, "staged"), 1)
                return body

            def tile_stats(phase):
                def body(t, s, used):
                    hold(dve, *after(phase, "kept", t + 1))
                    n = LAST if isinstance(t, int) and t == T - 1 else P
                    for h in range(DH):
                        last = nc.vector.bn_stats(stats[:, h, ds(t * 6, 6)], H[:, ds(t * D + h * P, n)])
                    last.then_inc(psem(phase, "stats"), 1)
                return body

            def row_stats(phase):
                def body(t, s, used):
                    hold(dve, *after(phase, "v", t + 1))
                    nc.vector.bn_stats(ln_stats[:, ds(t * 6, 6)], tile(acc, t, DEGW)).then_inc(psem(phase, "row_stats"), 1)
                return body

            def third_part(t, s, used):
                dve.wait_ge(psem("h", "second"), t + 1)
                tt(parts[:, s, 2, :], rest[:, s, :], parts[:, s, 1, :], ALU.subtract).then_inc(psem("h", "parts"), 1)

            def left_of(phase, src):
                def body(t, s, used):
                    dve.wait_ge(*after(phase, "first", t + 1))
                    if used:
                        dve.wait_ge(*after(phase, "parts", t - 1))
                    tt(rest[:, s, :], src(t, s), parts[:, s, 0, :], ALU.subtract).then_inc(psem(phase, "left"), 1)
                return body

            def layer_norm(phase, n, scaled=False):
                st = ln_stats.rearrange("p (t c) -> p t c", c=6)
                tt(mean[:, :], st[:, :, 1], st[:, :, 4], ALU.add)
                tt(ln_w[:, 0, :], st[:, :, 1], st[:, :, 4], ALU.subtract)
                link(tt(ln_w[:, 1, :], st[:, :, 2], st[:, :, 5], ALU.add))
                ts(mean[:, :], mean[:, :], 0.5, None, ALU.mult)
                link(stt(ln_w[:, 2, :], ln_w[:, 0, :], 0.25, ln_w[:, 0, :], ALU.mult, ALU.mult))
                link(stt(rstd[:, :], ln_w[:, 1, :], 1.0 / D, ln_w[:, 2, :], ALU.mult, ALU.add))
                link(ts(rstd[:, :], rstd[:, :], EPS, None, ALU.add))
                dve.sem_inc(ln_var, 1)
                dve.wait_ge(ln_std, n)
                link(nc.vector.reciprocal(rstd[:, :], std[:, :]))
                if n == 3:
                    link(ts(dis_r[:, :], acc[:, :].rearrange("p (t d) -> p t d", d=DEGW)[:, :, D], 1.0, None, ALU.add))
                    dve.sem_inc(ln_var, 1)
                    dve.wait_ge(ln_std, n + 1)
                    link(nc.vector.reciprocal(dis[:, :], dis[:, :]))

                def normal(t, s, used):
                    ts(tile(X, t), tile(acc, t, DEGW), mean[:, ds(t, 1)], rstd[:, ds(t, 1)], ALU.subtract, ALU.mult)\
                        .then_inc(psem(phase, "x" if scaled else "rows"), 1)

                def scale(t, s, used):
                    dve.wait_ge(*after(phase, "x", t + 1))
                    ts(tile(H, t), tile(X, t), dis[:, ds(t, 1)], None, ALU.mult).then_inc(psem(phase, "rows"), 1)

                if scaled:
                    over_tiles(dve, (normal, 0), (scale, 1), (left_of(phase, lambda t, s: tile(H, t)), 3))
                else:
                    over_tiles(dve, normal)
                dve.wait_ge(*after(phase, "rows", T))
                nc.vector.memset(acc[:, :], 0.0)

            nc.vector.memset(ends["dst"], NO_TILE)
            nc.vector.memset(ends["src"], NO_TILE)
            nc.vector.memset(X[:, (T - 1) * D:T * D], 0.0)
            link(nc.vector.memset(weight, 0.0))
            dve.sem_inc(fills, 1)
            link(nc.vector.memset(rec[:, :], 0.0))
            link(nc.vector.memset(rec_v[:, :, 1], -1.0))
            dve.sem_inc(fills, 1)
            dve.wait_ge(counts, 2)
            dve.wait_ge(edges_in, 96)
            dve.wait_ge(psem("sort", "padded"), 1)
            link(nc.vector.tensor_copy(iota_bf[:, :], iota_row[:, :]))
            sort(0)
            records(0)
            barrier(dve, 1)

            over_tiles(dve, (stage_tile("y", lambda t: tile(X, t)), 0), (tile_stats("y"), 2))
            dve.wait_ge(psem("y", "stats"), T)
            batch_norm(1, pcol[:, 1, :], pcol[:, 2, :])
            dve.sem_inc(vars_in, 1)

            def h_tile(t, s, used):
                if used:
                    dve.wait_ge(psem("h", "left"), t - 1)
                hold(dve, psem("h", "turned"), t + 1)
                nc.vector.tensor_copy(nm[:, s, :], bank[2 + s][:, 0:D]).then_inc(psem("h", "rows"), 1)
            over_tiles(dve, (h_tile, 0), (left_of("h", lambda t, s: nm[:, s, :]), 1), (third_part, 2))
            sort(1)
            barrier(dve, 2)
            records(1)
            barrier(dve, 3)
            barrier(dve, 4)
            nc.vector.memset(GP[:, :, PARTS * D], 1.0)
            link(nc.vector.memset(acc[:, :], 0.0))
            dve.sem_inc(summed, RING)
            dve.sem_inc(added, RING + 1)
            add_chunks(0)
            barrier(dve, 5)

            def conv_keep(t, s, used):
                dve.wait_ge(psem("conv", "product"), t + 1)
                for h in range(DH):
                    last = ts(H[:, ds(t * D + h * P, P)], bank[4 + s][:, h * P:(h + 1) * P], pcol[:, 4, h:h + 1], None, ALU.add)
                last.then_inc(psem("conv", "kept"), 1)
            over_tiles(dve, (stage_tile("conv", lambda t: tile(acc, t, DEGW)), 0), (conv_keep, 3), (tile_stats("conv"), 4))
            dve.wait_ge(psem("conv", "stats"), T)
            batch_norm(2, pcol[:, 5, :], pcol[:, 6, :])
            dve.sem_inc(vars_in, 1)

            def z_tile(t, s, used):
                dve.wait_ge(psem("z", "turned"), t + 1)
                stt(tile(acc, t, DEGW), tile(X, t), 2.0, bank[6 + s][:, 0:D], ALU.mult, ALU.add).then_inc(psem("z", "v"), 1)
            over_tiles(dve, (z_tile, 0), (row_stats("z"), 1))
            barrier(dve, 6)
            layer_norm("ln0", 3)
            barrier(dve, 7)
            add_chunks(1)
            barrier(dve, 8)

            def lin1_add(t, s, used):
                dve.wait_ge(psem("lin1", "product"), t + 1)
                tt(tile(acc, t, DEGW), bank[2 + s][:, 0:D], tile(X, t), ALU.add).then_inc(psem("lin1", "v"), 1)
            over_tiles(dve, (stage_tile("lin1", lambda t: tile(acc, t, DEGW)), 0), (lin1_add, 2), (row_stats("lin1"), 3))
            barrier(dve, 9)
            layer_norm("ln1", 5, scaled=True)
            barrier(dve, 10)
            add_chunks(2)
            barrier(dve, 11)

            def gcn_stage(phase):
                def body(t, s, used):
                    if used:
                        dve.wait_ge(*after(phase, "turned", t - 1))
                    tt(stg[:, s, :], tile(acc, t, DEGW), tile(H, t), ALU.add).then_inc(psem(phase, "staged"), 1)
                return body

            def gcn_bias(phase, i, reader):
                def body(t, s, used):
                    dve.wait_ge(*after(phase, "product", t + 1))
                    if used:
                        dve.wait_ge(*after(phase, reader, t - 1))
                    stt(gT[:, s, :], bank[2 + s][:, 0:D], dis[:, ds(t, 1)], bias[:, i, :], ALU.mult, ALU.add)\
                        .then_inc(psem(phase, "taken"), 1)
                return body

            def gcn_rows(phase):
                def body(t, s, used):
                    dve.wait_ge(*after(phase, "gelu", t + 1))
                    ts(tile(H, t), hT[:, s, :], dis[:, ds(t, 1)], None, ALU.mult).then_inc(psem(phase, "rows"), 1)
                return body

            def gcn_layer(phase, i):
                over_tiles(dve, (gcn_stage(phase), 0), (gcn_bias(phase, i, "gelu"), 2), (gcn_rows(phase), 3),
                           (left_of(phase, lambda t, s: tile(H, t)), 4))

            gcn_layer("gcn0", 0)
            link(nc.vector.memset(acc[:, :], 0.0))
            barrier(dve, 12)
            add_chunks(3)
            barrier(dve, 13)
            gcn_layer("gcn1", 1)
            link(nc.vector.memset(acc[:, :], 0.0))
            barrier(dve, 14)
            add_chunks(4)
            barrier(dve, 15)

            def gcn2_add(t, s, used):
                dve.wait_ge(*after("gcn2", "taken", t + 1))
                tt(tile(acc, t, DEGW), gT[:, s, :], tile(X, t), ALU.add).then_inc(psem("gcn2", "v"), 1)
            over_tiles(dve, (gcn_stage("gcn2"), 0), (gcn_bias("gcn2", 2, "v"), 2), (gcn2_add, 3), (row_stats("gcn2"), 4))
            barrier(dve, 16)
            layer_norm("ln2", 6)
            barrier(dve, 17)
            add_chunks(5)
            barrier(dve, 18)
            fixed_norm(7, pcol[:, 3, :], pcol[:, 4, :], pcol[:, 1, :], pcol[:, 2, :])
            dve.wait_ge(psem("norm2", "in"), 16 * 4)
            link(ts(H[:, 3 * D:4 * D], H[:, 3 * D:4 * D], EPS, None, ALU.add))
            dve.sem_inc(ln_var, 1)
            dve.wait_ge(ln_std, 8)
            link(nc.vector.reciprocal(bias[:, 3, :], bias[:, 3, :]))
            link(tt(bias[:, 1, :], bias[:, 3, :], H[:, 0:D], ALU.mult))
            link(tt(bias[:, 2, :], H[:, 2 * D:3 * D], bias[:, 1, :], ALU.mult))
            link(tt(bias[:, 2, :], H[:, D:2 * D], bias[:, 2, :], ALU.subtract))
            barrier(dve, 19)

            def ffn_stage(t, s, used):
                if used:
                    dve.wait_ge(psem("ffn", "turned"), t - 1)
                stt(stg[:, s, :], tile(X, t), 2.0, tile(acc, t, DEGW), ALU.mult, ALU.add).then_inc(psem("ffn", "staged"), 1)
                dve.wait_ge(psem("ffn", "staged"), t + 1)
                ts(tile(acc, t, DEGW), stg[:, s, :], 1.0, None, ALU.mult).then_inc(psem("ffn", "h"), 1)

            def ffn_add(t, s, used):
                dve.wait_ge(psem("ffn", "product"), t + 1)
                dve.wait_ge(psem("ffn", "h"), t + 1)
                if used:
                    dve.wait_ge(psem("ffn", "scaled"), t - 1)
                tt(nm[:, s, :], bank[4 + s][:, 0:D], tile(acc, t, DEGW), ALU.add).then_inc(psem("ffn", "taken"), 1)

            def ffn_scale(t, s, used):
                dve.wait_ge(psem("ffn", "taken"), t + 1)
                if used:
                    dve.wait_ge(psem("ffn", "v"), t - 1)
                tt(rest[:, s, :], nm[:, s, :], bias[:, 1, :], ALU.mult).then_inc(psem("ffn", "scaled"), 1)

            def ffn_shift(t, s, used):
                dve.wait_ge(psem("ffn", "scaled"), t + 1)
                tt(rest[:, s, :], rest[:, s, :], bias[:, 2, :], ALU.add).then_inc(psem("ffn", "shifted"), 1)

            def ffn_v(t, s, used):
                dve.wait_ge(psem("ffn", "shifted"), t + 1)
                tt(tile(acc, t, DEGW), rest[:, s, :], tile(X, t), ALU.add).then_inc(psem("ffn", "v"), 1)
            over_tiles(dve, (ffn_stage, 0), (ffn_add, 3), (ffn_scale, 4), (ffn_shift, 5), (ffn_v, 5), (row_stats("ffn"), 6))
            barrier(dve, 20)
            layer_norm("ln3", 9)
            barrier(dve, 21)


_INS = ["x", "src", "dst", "edge_attr_256", "edge_weight",
        "L0_gnn_w1", "L0_gnn_b1", "L0_gnn_g1", "L0_gnn_beta1", "L0_gnn_wr", "L0_gnn_br", "L0_gnn_wroot",
        "L0_gnn_w2", "L0_gnn_b2", "L0_gnn_g2", "L0_gnn_beta2", "L1_gnn_W", "L1_gnn_b",
        "L2_gnn_W1", "L2_gnn_b1", "L2_gnn_W2", "L2_gnn_b2", "L2_gnn_W3", "L2_gnn_b3",
        "L3_gnn_W1", "L3_gnn_b1", "L3_gnn_W2", "L3_gnn_b2",
        "L3_gnn_bn1_gamma", "L3_gnn_bn1_beta", "L3_gnn_bn1_mean", "L3_gnn_bn1_var",
        "L3_gnn_bn2_gamma", "L3_gnn_bn2_beta", "L3_gnn_bn2_mean", "L3_gnn_bn2_var"]


def kernel(**inputs):
    import numpy as _np
    import concourse.bacc as _bacc
    from concourse import mybir as _mybir
    from concourse.bass_utils import run_bass_kernel_spmd as _run

    nc = _bacc.Bacc("TRN2", target_bir_lowering=False, num_devices=1)
    arrays, args = {}, {}
    for name in _INS:
        arr = _np.ascontiguousarray(inputs[name])
        arrays[f"in_{name}_dram"] = arr
        args[name] = nc.dram_tensor(f"in_{name}_dram", arr.shape, _mybir.dt.from_np(arr.dtype), kind="ExternalInput").ap()
    n, d = inputs["x"].shape
    out = nc.dram_tensor("out_0_dram", (n, d), _mybir.dt.float32, kind="ExternalOutput").ap()
    gnn_kernel(nc, args, out)
    r = _run(nc, [arrays], core_ids=[0])
    return r.results[0]["out_0_dram"]
```

```python
from contextlib import ExitStack

import concourse.bass as bass
from concourse import mybir

P = 128
ALU = mybir.AluOpType
ACT = mybir.ActivationFunctionType
F32 = mybir.dt.float32
I32 = mybir.dt.int32
BF16 = mybir.dt.bfloat16
EPS = 1e-5
ds = bass.ds

RING = 16
BATCH = 4
ONEHOTS = 8
MSGS = 8
SUMS = 4
PARTS = 3
PSLOTS = 4
REC = 3


def gnn_kernel(nc, a, out):
    N, D = a["x"].shape
    E = a["src"].shape[0]
    T = -(-N // P)
    LAST = N - (T - 1) * P
    NP = T * P
    C = -(-(E + T * (P - 1)) // (P * RING)) * RING
    FE = -(-E // (P * RING)) * RING
    PFULL = E // FE
    REST = E - PFULL * FE
    DH = D // P
    DEGW = D + 1
    RINGW = PARTS * D // 2 + 1
    NO_TILE = P * (T + 1)
    assert DH == 2 and PFULL == P - 1 and REST > 0 and T < 64

    rec_dram = {k: nc.dram_tensor(f"records_by_{k}", (P * C + FE, REC), F32).ap() for k in ("dst", "src")}
    plain_records = nc.dram_tensor("plain_records", (P * FE, REC), F32).ap()
    starts_dram = nc.dram_tensor("chunk_starts", (1, C), I32).ap()
    tiles_dram = {k: nc.dram_tensor(f"tile_of_chunk_by_{k}", (1, C), I32).ap() for k in ("dst", "src")}
    table = {k: nc.dram_tensor(f"table_{k}", (NP, D), F32).ap() for k in ("x1", "x3")}
    table |= {k: nc.dram_tensor(f"table_{k}", (NP, PARTS * D), BF16).ap() for k in ("h", "g0", "g1", "g2")}

    with ExitStack() as ctx:
        def sb(name, shape, dt=F32):
            return ctx.enter_context(nc.sbuf_tensor(name, shape, dt))

        def sem(name):
            return ctx.enter_context(nc.semaphore(name))

        bank = [ctx.enter_context(nc.psum_tensor(f"bank{i}", [P, 512], F32)) for i in range(8)]

        X = sb("X", [P, T * D])
        H = sb("H", [P, T * D])
        acc = sb("acc", [P, T * DEGW])
        rec = sb("rec", [P, C * REC])
        tile_row = sb("tile_row", [1, C], I32)
        ring_mem = sb("ring_mem", [P, RING * RINGW])
        idx_ring = sb("idx_ring", [P, RING], I32)
        eid_ring = sb("eid_ring", [P, RING], I32)
        onehot = sb("onehot", [P, ONEHOTS, P])
        onehot_bf = onehot[:, :, :].rearrange("p s j -> p (s j)").bitcast(BF16)\
            .rearrange("p (s j) -> p s j", s=ONEHOTS)[:, :, 0:P]
        rec_v = rec[:, :].rearrange("p (c w) -> p c w", w=REC)
        G = ring_mem[:, 0:RING * D].rearrange("p (s d) -> p s d", s=RING)
        GP = ring_mem[:, :].bitcast(BF16).rearrange("p (s d) -> p s d", s=RING)
        EA = H[:, 0:RING * D].rearrange("p (s d) -> p s d", s=RING)
        M = H[:, RING * D:(RING + MSGS) * D].rearrange("p (s d) -> p s d", s=MSGS)

        iota_row = sb("iota_row", [P, P])
        ident = sb("ident", [P, P])
        below = sb("below", [P, P])
        upto = sb("upto", [P, P])
        ones = sb("ones", [P, P])

        wt = {k: sb(f"wt_{k}", [P, DH, D]) for k in ("a", "b", "c", "d")}
        pcol = sb("pcol", [P, 9, DH])
        bias = sb("bias", [P, 4, D])
        stats = sb("stats", [P, DH, T * 6])
        ln_stats = stats[:, 0, :]
        ln_w = sb("ln_w", [P, 3, T])
        mean = sb("mean", [P, T])
        std = sb("std", [P, T])
        rstd = sb("rstd", [P, T])
        dis_r = sb("dis_r", [P, T])
        dis = sb("dis", [P, T])
        bn_mv = sb("bn_mv", [P, DH, 2])
        bn_s = sb("bn_s", [P, 4, DH])

        def stage(i):
            return ring_mem[:, 2 * i * D:2 * (i + 1) * D].rearrange("p (s d) -> p s d", s=2)

        stg, fT, hT, gT, nm, rest = (stage(i) for i in range(6))
        parts = ring_mem[:, 12 * D:12 * D + PSLOTS * PARTS * D // 2].bitcast(BF16)\
            .rearrange("p (s q d) -> p s q d", s=PSLOTS, q=PARTS)

        cnt = ring_mem[:, 16 * D:16 * D + 6 * 64].rearrange("p (w t) -> p w t", w=6)
        cnt_i = ring_mem[:, 18 * D:18 * D + 2 * 64].bitcast(I32).rearrange("p (w t) -> p w t", w=2)

        pad_rows = ring_mem[:, 18 * D + 2 * 64:19 * D]
        start_row = ring_mem[0:1, 19 * D:19 * D + C].bitcast(I32)
        unsorted = sb("unsorted", [1, 1], I32)
        sorted_f = sb("sorted_f", [P, 1])

        def acc_cols(i, n=1, dt=F32):
            part = acc[:, i * FE:(i + n) * FE]
            return part if dt == F32 else part.bitcast(dt)

        ends = {"dst": acc_cols(0, 1, I32), "src": acc_cols(1, 1, I32)}
        weight = acc_cols(2)
        key = acc_cols(3)
        scan = acc_cols(4)
        mask = acc_cols(5)
        tmp_i = acc_cols(6, 1, I32)
        slot_f = acc_cols(7)
        slot_i = {"dst": acc_cols(8, 1, I32), "src": acc_cols(9, 1, I32)}
        rec_e = acc_cols(10, REC)
        dst_next = slot_i["dst"]
        first_edge = acc[:, (10 + REC) * FE:(10 + REC) * FE + C]
        tile_base = acc[:, (10 + REC) * FE + C:(10 + REC) * FE + 2 * C]
        chunk_no = rec[:, 0:C]
        chunk_cmp = rec[:, C:2 * C]
        plain_e = H[:, 4 * DH * D:4 * DH * D + FE * REC]
        plain_ev = plain_e.rearrange("p (f w) -> p f w", w=REC)
        edge_no = plain_ev[:, :, 2]
        rec_ev = rec_e.rearrange("p (f w) -> p f w", w=REC)
        scan_i = scan.bitcast(I32)
        mask_i = mask.bitcast(I32)
        idx_stage = idx_ring
        rec_stage = sb("rec_stage", [P, RING, REC])
        rec_stage_flat = rec_stage[:, :, :].rearrange("p s w -> p (s w)")
        assert (10 + REC) * FE + 2 * C <= T * DEGW and 19 * D + C <= RING * RINGW and E >= P
        wnat = H[:, 0:4 * DH * D].rearrange("p (q h d) -> p q h d", q=4, h=DH)

        phase_end = sem("phase_end")
        spaced = sem("spaced")
        gathered = [sem(f"gathered{i}") for i in range(RING // BATCH)]
        ea_in = [sem(f"ea_in{i}") for i in range(RING // BATCH)]
        scattered = {k: [sem(f"scattered_by_{k}{i}") for i in range(RING // BATCH)] for k in ("dst", "src")}
        staged = {k: sem(f"staged_by_{k}") for k in ("dst", "src")}
        idx_ready = sem("idx_ready")
        summed = sem("summed")
        onehot_ready = sem("onehot_ready")
        onehot_raw = sem("onehot_raw")
        added = sem("added")
        msg_added = sem("msg_added")
        msg_relu = sem("msg_relu")
        vec_chain = sem("vec_chain")
        act_chain = sem("act_chain")
        pool_chain = sem("pool_chain")
        loads = sem("loads")
        edges_in = sem("edges_in")
        stores = sem("stores")
        fills = sem("fills")
        sorts = sem("sorts")
        constants_ready = sem("constants_ready")
        w_in = sem("w_in")
        w_turned = sem("w_turned")
        w_copied = sem("w_copied")
        ln_var = sem("ln_var")
        ln_std = sem("ln_std")
        vars_in = sem("vars_in")

        made = {}

        def psem(phase, what):
            name = "gcn" if phase in ("gcn0", "gcn1") else phase
            if (name, what) not in made:
                made[name, what] = sem(f"{name}_{what}")
            return made[name, what]

        def slot_tiles(s):
            return -(-(T - s) // PSLOTS)

        def after(phase, what, n):
            each = slot_tiles(int(what[-1])) * 16 if what[:-1] == "written" else T
            return psem(phase, what), n + (each if phase == "gcn1" else 0)

        block = ctx.enter_context(nc.Block())

        def barrier(eng, k):
            eng.drain().then_inc(phase_end, 1)
            eng.wait_ge(phase_end, 5 * k)

        def hold(eng, sm, value):
            eng.wait_ge(sm, value)
            if not isinstance(value, int):
                eng.sem_inc(spaced, 1)

        def over_tiles(eng, *stages):
            stages = [st if isinstance(st, tuple) else (st, 0) for st in stages]
            stages = [st if len(st) == 3 else (*st, 2) for st in stages]
            most = max(lag for _, lag, _ in stages)
            turns = max(slots for _, _, slots in stages)
            first = -(-(most + turns) // turns) * turns
            rounds = (T - 1 - first) // turns

            def step(t, turn):
                for f, lag, slots in stages:
                    if not isinstance(t, int) or 0 <= t - lag < T:
                        f(t - lag, (turn - lag) % slots, not isinstance(t, int) or t - lag >= slots)

            for t in range(first):
                step(t, t)
            with eng.Fori(0, rounds) as i:
                for j in range(turns):
                    step(i * turns + (first + j), j)
            for t in range(first + rounds * turns, T + most):
                step(t, t)

        def later(t, n):
            return not isinstance(t, int) or t >= n

        def edge_features(eng, i, s):
            start = eng.value_load(start_row[0:1, ds(i * RING + s, 1)], min_val=0, max_val=E - P)
            eng.dma_start(EA[:, s, :], a["edge_attr_256"][ds(start, P), :]).then_inc(ea_in[s // BATCH], 16)

        def take_records(eng, who):
            half = C // 2 * ("sp", "act").index(who)
            disorder = eng.value_load(unsorted[0:1, 0:1], min_val=0, max_val=E)
            with eng.If(disorder == 0):
                with eng.Fori(half // BATCH, (half + C // 2) // BATCH) as i:
                    for j in range(BATCH):
                        start = eng.value_load(start_row[0:1, ds(i * BATCH + j, 1)], min_val=0, max_val=E - P)
                        with nc.allow_non_contiguous_dma(reason="a record a partition"):
                            eng.dma_start(rec[:, ds((i * BATCH + j) * REC, REC)], plain_records[ds(start, P), :])\
                               .then_inc(psem("records", f"taken_{who}"), 16)
                eng.wait_ge(psem("records", f"taken_{who}"), 16 * (C // 2))

        def tile(buf, t, width=D, cols=D):
            return buf[:, ds(t * width, cols)]

        AGGS = [("dst", "h", False, True, False), ("src", "x1", True, False, False),
                ("dst", "g0", False, False, False), ("dst", "g1", False, False, False),
                ("dst", "g2", False, False, False), ("dst", "x3", False, False, True)]

        @block.sync
        def _(sp):
            total = {"loads": 0, "stores": 0}

            def load(dst, src, sm=loads, name="loads"):
                sp.dma_start(dst, src).then_inc(sm, 16)
                if name in total:
                    total[name] += 16

            def loaded():
                sp.wait_ge(loads, total["loads"])

            def store(dst, src):
                sp.dma_start(dst, src).then_inc(stores, 16)
                total["stores"] += 16

            def columns(i, name):
                with nc.allow_non_contiguous_dma(reason="256 words"):
                    load(pcol[:, i, :], a[name].rearrange("(h p) -> p h", p=P))

            def bias_row(i, name):
                load(bias[:, i, :], a[name].rearrange("(o d) -> o d", o=1).to_broadcast((P, D)))

            def weights(k, name):
                load(wt[k][:, :, :], a[name].rearrange("(h k) n -> k h n", k=P))

            def natural_weights(names):
                for q, name in enumerate(names):
                    sp.dma_start(wnat[:, q, :, :], a[name].rearrange("(h o) k -> o h k", o=P)).then_inc(w_in, 16)

            def write_table(phase, buf, name):
                def body(t, s, used):
                    sp.wait_ge(*after(phase, "rows", t + 1))
                    sp.dma_start(table[name][ds(t * P, P), :], tile(buf, t)).then_inc(psem(phase, "written"), 16)
                over_tiles(sp, body)
                sp.wait_ge(*after(phase, "written", 16 * T))

            def write_parts(phase, name):
                def body(t, s, used):
                    sp.wait_ge(*after(phase, "parts", t + 1))
                    sp.dma_start(table[name][ds(t * P, P), :], parts[:, s, :, :].rearrange("p q d -> p (q d)"))\
                      .then_inc(psem(phase, f"written{s}"), 16)
                over_tiles(sp, (body, 0, PSLOTS))
                for s in range(PSLOTS):
                    sp.wait_ge(*after(phase, f"written{s}", 16 * slot_tiles(s)))

            def load_records(which):
                load(rec[:, :], rec_dram[which][0:P * C, :].rearrange("(p c) w -> p (c w)", p=P))
                load(tile_row[:, :], tiles_dram[which])
                loaded()

            sp.wait_ge(fills, 1)
            for k in ("dst", "src"):
                sp.dma_start(ends[k][0:PFULL, :], a[k][0:PFULL * FE].rearrange("(p f) -> p f", p=PFULL)).then_inc(edges_in, 16)
                sp.dma_start(ends[k][PFULL:P, 0:REST], a[k][PFULL * FE:E].rearrange("(p f) -> p f", p=1)).then_inc(edges_in, 16)
            sp.dma_start(dst_next[0:PFULL, :], a["dst"][1:PFULL * FE + 1].rearrange("(p f) -> p f", p=PFULL)).then_inc(edges_in, 16)
            sp.dma_start(dst_next[PFULL:P, 0:REST - 1], a["dst"][PFULL * FE + 1:E].rearrange("(p f) -> p f", p=1)).then_inc(edges_in, 16)
            sp.dma_start(weight[0:PFULL, :], a["edge_weight"][0:PFULL * FE].rearrange("(p f) -> p f", p=PFULL)).then_inc(edges_in, 16)
            sp.dma_start(weight[PFULL:P, 0:REST], a["edge_weight"][PFULL * FE:E].rearrange("(p f) -> p f", p=1)).then_inc(edges_in, 16)
            natural_weights(("L0_gnn_w1", "L0_gnn_wr", "L0_gnn_wroot", "L0_gnn_w2"))
            for i, name in enumerate(("b1", "g1", "beta1", "br", "b2", "g2", "beta2")):
                columns(i, "L0_gnn_" + name)
            load(X[:, 0:(T - 1) * D].rearrange("p (t d) -> p t d", d=D),
                 a["x"][0:(T - 1) * P, :].rearrange("(t p) d -> p t d", p=P))
            load(X[0:LAST, (T - 1) * D:T * D], a["x"][(T - 1) * P:N, :])
            sp.wait_ge(fills, 2)
            for k in ("dst", "src"):
                store(rec_dram[k][0:P * C, :].rearrange("(p c) w -> p (c w)", p=P), rec[:, :])
            sp.wait_ge(stores, total["stores"])
            sp.sem_inc(psem("sort", "padded"), 1)
            sp.wait_ge(psem("sort", "tiles"), 1)
            store(tiles_dram["src"], tile_row[:, :])
            sp.wait_ge(stores, total["stores"])
            sp.sem_inc(psem("sort", "tile_row_free"), 1)
            loaded()
            barrier(sp, 1)
            sp.wait_ge(psem("sort", "tiles"), 2)
            store(tiles_dram["dst"], tile_row[:, :])
            store(starts_dram, start_row)
            sp.wait_ge(psem("sort", "records"), 1)
            store(plain_records.rearrange("(p f) w -> p (f w)", p=P), plain_e)
            sp.wait_ge(stores, total["stores"])
            sp.sem_inc(psem("records", "stored"), 1)
            take_records(sp, "sp")
            write_parts("h", "h")
            barrier(sp, 2)
            disorder = sp.value_load(unsorted[0:1, 0:1], min_val=0, max_val=E)
            with sp.If(disorder > 0):
                sp.dma_start(rec_e, plain_records.rearrange("(p f) w -> p (f w)", p=P)).then_inc(psem("records", "back"), 16)
                sp.wait_ge(psem("records", "scattered"), 1)
                sp.dma_start(rec[:, :], rec_dram["dst"][0:P * C, :].rearrange("(p c) w -> p (c w)", p=P))\
                  .then_inc(psem("records", "loaded"), 16)
                sp.wait_ge(psem("records", "loaded"), 16)
            barrier(sp, 3)
            barrier(sp, 4)
            store(rec_dram["dst"][0:P * C, :].rearrange("(p c) w -> p (c w)", p=P), rec[:, :])
            sp.wait_ge(stores, total["stores"])
            barrier(sp, 5)
            barrier(sp, 6)
            load_records("src")
            weights("a", "L1_gnn_W")
            bias_row(0, "L1_gnn_b")
            loaded()
            write_table("ln0", X, "x1")
            barrier(sp, 7)
            barrier(sp, 8)
            load_records("dst")
            barrier(sp, 9)
            weights("a", "L2_gnn_W1")
            weights("b", "L2_gnn_W2")
            weights("c", "L2_gnn_W3")
            for i in range(3):
                bias_row(i, f"L2_gnn_b{i + 1}")
            loaded()
            write_parts("ln1", "g0")
            barrier(sp, 10)
            barrier(sp, 11)
            write_parts("gcn0", "g1")
            barrier(sp, 12)
            barrier(sp, 13)
            write_parts("gcn1", "g2")
            barrier(sp, 14)
            barrier(sp, 15)
            barrier(sp, 16)
            natural_weights(("L3_gnn_W1", "L3_gnn_W2"))
            bias_row(0, "L3_gnn_b2")
            for i, name in enumerate(("b1", "bn1_gamma", "bn1_beta", "bn1_mean", "bn1_var")):
                columns(i, "L3_gnn_" + name)
            loaded()
            write_table("ln2", X, "x3")
            load(start_row, starts_dram)
            loaded()
            barrier(sp, 17)
            disorder = sp.value_load(unsorted[0:1, 0:1], min_val=0, max_val=E)
            with sp.If(disorder == 0):
                with sp.Fori(0, C // RING) as i:
                    for s in range(RING):
                        if s % BATCH == 0:
                            hold(sp, msg_added, i * (RING // BATCH) + s // BATCH + 1)
                        if s % BATCH < BATCH - 1:
                            edge_features(sp, i, s)
            barrier(sp, 18)
            for i, name in enumerate(("gamma", "beta", "mean", "var")):
                sp.dma_start(H[:, i * D:(i + 1) * D], a["L3_gnn_bn2_" + name].rearrange("(o d) -> o d", o=1)
                             .to_broadcast((P, D))).then_inc(psem("norm2", "in"), 16)
            sp.wait_ge(psem("norm2", "in"), 64)
            barrier(sp, 19)
            barrier(sp, 20)

            def out_rows(t, s, used):
                sp.wait_ge(psem("ln3", "rows"), t + 1)
                if isinstance(t, int) and t == T - 1:
                    sp.dma_start(out[t * P:N, :], X[0:LAST, t * D:(t + 1) * D]).then_inc(psem("ln3", "written"), 16)
                else:
                    sp.dma_start(out[ds(t * P, P), :], tile(X, t)).then_inc(psem("ln3", "written"), 16)
            over_tiles(sp, out_rows)
            sp.wait_ge(psem("ln3", "written"), 16 * T)
            barrier(sp, 21)

        @block.gpsimd
        def _(pool):
            chain = [0]

            def link(ins):
                chain[0] += 1
                ins.then_inc(pool_chain, 1)
                pool.wait_ge(pool_chain, chain[0])

            nc.gpsimd.iota(iota_row[:, :], [[1, P]], 0, channel_multiplier=0, allow_small_or_imprecise_dtypes=True)
            nc.gpsimd.memset(ones[:, :], 1.0)
            link(nc.gpsimd.memset(ident[:, :], 0.0))
            nc.gpsimd.affine_select(out=ident[:, :], in_=ident[:, :], compare_op=ALU.not_equal, fill=1.0,
                                    base=0, pattern=[[-1, P]], channel_multiplier=1).then_inc(constants_ready, 1)
            pool.wait_ge(pool_chain, 1)
            link(nc.gpsimd.affine_select(out=below[:, :], in_=ones[:, :], compare_op=ALU.is_gt, fill=0.0,
                                         base=0, pattern=[[1, P]], channel_multiplier=-1))
            link(nc.gpsimd.affine_select(out=upto[:, :], in_=ones[:, :], compare_op=ALU.is_ge, fill=0.0,
                                         base=0, pattern=[[1, P]], channel_multiplier=-1))
            link(nc.gpsimd.iota(edge_no, [[1, FE]], 0, channel_multiplier=FE, allow_small_or_imprecise_dtypes=True))
            pool.sem_inc(constants_ready, 1)

            def scatter(which):

                def body(i):
                    for g in range(RING // BATCH):
                        at = i * RING + g * BATCH
                        if not (isinstance(i, int) and i == 0):
                            hold(pool, scattered[which][g], i * (16 * BATCH))
                        nc.gpsimd.tensor_copy(idx_stage[:, g * BATCH:(g + 1) * BATCH], slot_i[which][:, ds(at, BATCH)])
                        nc.gpsimd.tensor_copy(rec_stage_flat[:, g * BATCH * REC:(g + 1) * BATCH * REC],
                                              rec_e[:, ds(at * REC, BATCH * REC)]).then_inc(staged[which], 1)
                        hold(pool, staged[which], i * (RING // BATCH) + g + 1)
                        for j in range(g * BATCH, (g + 1) * BATCH):
                            pool.indirect_dma_start(
                                out=rec_dram[which][:, :], out_offset=bass.IndirectOffsetOnAxis(ap=idx_stage[:, j:j + 1], axis=0),
                                in_=rec_stage[:, j, :], in_offset=None).then_inc(scattered[which][g], 16)
                body(0)
                with pool.Fori(1, FE // RING) as i:
                    body(i)
                for g in range(RING // BATCH):
                    pool.wait_ge(scattered[which][g], 16 * BATCH * (FE // RING))

            def third_parts(phase):
                def body(t, s, used):
                    hold(pool, *after(phase, "second", t + 1))
                    nc.gpsimd.tensor_tensor(parts[:, s, 2, :], rest[:, s % 2, :], parts[:, s, 1, :], ALU.subtract)\
                      .then_inc(psem(phase, "parts"), 1)
                over_tiles(pool, (body, 0, PSLOTS))

            def gather(n, edges=False):
                which, name, weighted, counted, messages = AGGS[n]
                rows = G if weighted or messages else GP[:, :, 0:PARTS * D]
                with pool.Fori(0, C // RING) as i:
                    for s in range(RING):
                        if s % BATCH == 0:
                            hold(pool, idx_ready, i * (RING // BATCH) + s // BATCH + 1 + n * (C // BATCH))
                        pool.indirect_dma_start(
                            out=rows[:, s, :], out_offset=None, in_=table[name][:, :],
                            in_offset=bass.IndirectOffsetOnAxis(ap=idx_ring[:, s:s + 1], axis=0)).then_inc(gathered[s // BATCH], 16)
                        if edges:
                            pool.indirect_dma_start(
                                out=EA[:, s, :], out_offset=None, in_=a["edge_attr_256"][:, :],
                                in_offset=bass.IndirectOffsetOnAxis(ap=eid_ring[:, s:s + 1], axis=0)).then_inc(ea_in[s // BATCH], 16)

            pool.wait_ge(psem("sort", "padded"), 1)
            nc.gpsimd.iota(chunk_no, [[1, C]], 0, channel_multiplier=0,
                           allow_small_or_imprecise_dtypes=True).then_inc(psem("sort", "chunk_no"), 1)
            barrier(pool, 1)
            scatter("src")
            barrier(pool, 2)
            disorder = pool.value_load(unsorted[0:1, 0:1], min_val=0, max_val=E)
            with pool.If(disorder > 0):
                pool.wait_ge(psem("records", "back"), 16)
                scatter("dst")
                pool.sem_inc(psem("records", "scattered"), 1)
            barrier(pool, 3)
            barrier(pool, 4)
            gather(0)
            barrier(pool, 5)
            barrier(pool, 6)
            barrier(pool, 7)
            gather(1)
            barrier(pool, 8)
            barrier(pool, 9)
            third_parts("ln1")
            barrier(pool, 10)
            gather(2)
            barrier(pool, 11)
            third_parts("gcn0")
            barrier(pool, 12)
            gather(3)
            barrier(pool, 13)
            third_parts("gcn1")
            barrier(pool, 14)
            gather(4)
            barrier(pool, 15)
            barrier(pool, 16)
            barrier(pool, 17)
            disorder = pool.value_load(unsorted[0:1, 0:1], min_val=0, max_val=E)
            with pool.If(disorder == 0):
                gather(5)
            with pool.Else():
                gather(5, edges=True)
            for k in range(18, 22):
                barrier(pool, k)

        @block.tensor
        def _(pe):
            def sum_chunks(n):
                which, name, weighted, counted, edges = AGGS[n]
                with pe.Fori(0, C // RING) as i:
                    for s in range(RING):
                        c = i * RING + s + n * C
                        sum_ = bank[s % SUMS]
                        if s % BATCH == 0:
                            pe.wait_ge(onehot_ready, i * (RING // BATCH) + s // BATCH + 1 + n * (C // BATCH))
                            if edges:
                                pe.wait_ge(msg_relu, i * (RING // BATCH) + s // BATCH + 1)
                            else:
                                pe.wait_ge(gathered[s // BATCH], (i + (n * (C // RING) + 1)) * (16 * BATCH))
                        pe.wait_ge(added, c + (RING + 2 - SUMS))
                        if weighted or edges:
                            rows = M[:, s % MSGS, :] if edges else G[:, s, :]
                            last = pe.matmul(sum_[:, 0:D], onehot[:, s % ONEHOTS, :], rows, start=True, stop=True)
                        else:
                            for q in reversed(range(PARTS)):
                                width = DEGW if counted and q == PARTS - 1 else D
                                last = pe.matmul(sum_[:, 0:width], onehot_bf[:, s % ONEHOTS, :],
                                                 GP[:, s, q * D:q * D + width], start=(q == PARTS - 1), stop=(q == 0),
                                                 skip_group_check=True)
                        last.then_inc(summed, 1)

            def turn(phase, src, to, s):
                for h in range(DH):
                    last = pe.transpose(to[:, h * P:(h + 1) * P], src[:, s, h * P:(h + 1) * P], ident[:, :])
                last.then_inc(psem(phase, "turned"), 1)

            def to_features(dst, pairs):
                for o in range(DH):
                    n = 0
                    for wk, val in pairs:
                        for k in range(DH):
                            last = pe.matmul(dst[:, o * P:(o + 1) * P], wk[:, k, o * P:(o + 1) * P],
                                             val[:, k * P:(k + 1) * P], start=(n == 0), stop=(n == DH * len(pairs) - 1))
                            n += 1
                return last

            def to_nodes(dst, wk, val, row=None):
                for k in range(DH):
                    last = pe.matmul(dst[:, 0:D], val[:, k * P:(k + 1) * P], wk[:, k, :], start=(k == 0),
                                     stop=(k == DH - 1 and row is None))
                if row is not None:
                    last = pe.matmul(dst[:, 0:D], ones[0:1, :], row, start=False, stop=True)
                return last

            def sort_counts(k):
                pe.wait_ge(sorts, 3 * k + 1)
                pe.matmul(bank[0][:, 0:T], below[:, :], cnt[:, 0, 0:T], start=True, stop=True)
                pe.matmul(bank[1][:, 0:T], ones[:, :], cnt[:, 0, 0:T], start=True, stop=True)
                if k == 1:
                    pe.matmul(bank[2][:, 1:2], ones[:, :], cnt[:, 5, 3:4], start=True, stop=True, skip_group_check=True)
                pe.matmul(bank[2][0:T, 0:1], cnt[:, 0, 0:T], ones[:, 0:1], start=True, stop=True,
                          skip_group_check=True).then_inc(psem("sort", "mm"), 1)
                pe.wait_ge(sorts, 3 * k + 2)
                pe.matmul(bank[3][0:T, 0:1], upto[0:T, 0:T], cnt[0:T, 5, 0:1], start=True, stop=True).then_inc(psem("sort", "mm"), 1)
                pe.wait_ge(sorts, 3 * k + 3)
                if k == 1:
                    pe.matmul(bank[2][:, 0:512], pad_rows[0:T, :], chunk_cmp[0:T, 0:512], start=True, stop=True)
                    pe.matmul(bank[3][:, 0:C - 512], pad_rows[0:T, :], chunk_cmp[0:T, 512:C], start=True, stop=True)
                pe.matmul(bank[0][:, 0:512], ones[0:T, :], chunk_cmp[0:T, 0:512], start=True, stop=True)
                pe.matmul(bank[1][:, 0:C - 512], ones[0:T, :], chunk_cmp[0:T, 512:C], start=True, stop=True).then_inc(psem("sort", "mm"), 1)

            def turn_weights(n, before):
                pe.wait_ge(w_in, 16 * (before + n))
                for q in range(n):
                    if q >= 2:
                        pe.wait_ge(w_copied, before + q - 1)
                    for k in range(DH):
                        for o in range(DH):
                            last = pe.transpose(bank[4 + q % 2][:, k * D + o * P:k * D + (o + 1) * P],
                                                wnat[:, q, o, k * P:(k + 1) * P], ident[:, :])
                    last.then_inc(w_turned, 1)

            pe.wait_ge(constants_ready, 2)
            turn_weights(4, 0)
            sort_counts(0)
            barrier(pe, 1)

            def turn_staged(phase, src, first_bank, ready, free):
                def body(t, s, used):
                    pe.wait_ge(*after(phase, ready, t + 1))
                    if used:
                        pe.wait_ge(*after(phase, free, t - 1))
                    turn(phase, src, bank[first_bank + s], s)
                return body

            sort_counts(1)

            def y_product(t, s, used):
                pe.wait_ge(psem("y", "fT"), t + 1)
                if used:
                    pe.wait_ge(psem("y", "kept"), t - 1)
                to_features(bank[6 + s], [(wt["a"], fT[:, s, :])]).then_inc(psem("y", "product"), 1)
            over_tiles(pe, (turn_staged("y", stg, 4, "staged", "fT"), 0), (y_product, 1))
            over_tiles(pe, turn_staged("h", hT, 2, "scaled", "rows"))
            barrier(pe, 2)
            barrier(pe, 3)
            barrier(pe, 4)
            sum_chunks(0)
            barrier(pe, 5)

            def conv_mid(t, s, used):
                pe.wait_ge(psem("conv", "hT"), t + 1)
                pe.wait_ge(psem("conv", "fT"), t + 1)
                if used:
                    pe.wait_ge(psem("conv", "gT"), t - 1)
                to_features(bank[2 + s], [(wt["b"], fT[:, s, :]), (wt["c"], hT[:, s, :])]).then_inc(psem("conv", "mid"), 1)

            def conv_product(t, s, used):
                pe.wait_ge(psem("conv", "gT"), t + 1)
                if used:
                    pe.wait_ge(psem("conv", "kept"), t - 1)
                to_features(bank[4 + s], [(wt["d"], gT[:, s, :])]).then_inc(psem("conv", "product"), 1)
            over_tiles(pe, (turn_staged("conv", stg, 0, "staged", "fT"), 0), (conv_mid, 1), (conv_product, 2))
            over_tiles(pe, turn_staged("z", hT, 6, "scaled", "v"))
            barrier(pe, 6)
            barrier(pe, 7)
            sum_chunks(1)
            barrier(pe, 8)

            def linear(phase, wk, row, taken="taken"):
                def product(t, s, used):
                    pe.wait_ge(*after(phase, "fT", t + 1))
                    if used:
                        pe.wait_ge(*after(phase, taken, t - 1))
                    to_nodes(bank[2 + s], wk, fT[:, s, :], row).then_inc(psem(phase, "product"), 1)
                over_tiles(pe, (turn_staged(phase, stg, 0, "staged", "fT"), 0), (product, 1))

            linear("lin1", wt["a"], bias[0:1, 0, :], "v")
            barrier(pe, 9)
            barrier(pe, 10)
            sum_chunks(2)
            barrier(pe, 11)
            linear("gcn0", wt["a"], None)
            barrier(pe, 12)
            sum_chunks(3)
            barrier(pe, 13)
            linear("gcn1", wt["b"], None)
            barrier(pe, 14)
            sum_chunks(4)
            barrier(pe, 15)
            linear("gcn2", wt["c"], None)
            barrier(pe, 16)
            turn_weights(2, 4)
            barrier(pe, 17)
            sum_chunks(5)
            barrier(pe, 18)
            barrier(pe, 19)

            def ffn_mid(t, s, used):
                pe.wait_ge(psem("ffn", "fT"), t + 1)
                if used:
                    pe.wait_ge(psem("ffn", "gT"), t - 1)
                to_features(bank[2 + s], [(wt["a"], fT[:, s, :])]).then_inc(psem("ffn", "mid"), 1)

            def ffn_product(t, s, used):
                pe.wait_ge(psem("ffn", "gT"), t + 1)
                if used:
                    pe.wait_ge(psem("ffn", "taken"), t - 1)
                to_nodes(bank[4 + s], wt["b"], gT[:, s, :], bias[0:1, 0, :]).then_inc(psem("ffn", "product"), 1)
            over_tiles(pe, (turn_staged("ffn", stg, 0, "staged", "fT"), 0), (ffn_mid, 1), (ffn_product, 2))
            barrier(pe, 20)
            barrier(pe, 21)

        @block.scalar
        def _(act):
            def copy_turned(phase, s, t, used, reader, src, scale=None, shift=None):
                act.wait_ge(*after(phase, "turned", t + 1))
                if used:
                    hold(act, *after(phase, reader, t - 1))
                if scale is None:
                    nc.scalar.copy(fT[:, s, :], src[:, 0:D]).then_inc(psem(phase, "fT"), 1)
                else:
                    for h in range(DH):
                        last = nc.scalar.activation(fT[:, s, h * P:(h + 1) * P], src[:, h * P:(h + 1) * P], ACT.Identity,
                                                    bias=shift[:, h:h + 1], scale=scale[:, h:h + 1])
                    last.then_inc(psem(phase, "fT"), 1)

            def normed(phase, t, s, used, reader, what):
                if used:
                    hold(act, *after(phase, reader, t - 1))
                for h in range(DH):
                    last = nc.scalar.activation(hT[:, s, h * P:(h + 1) * P], H[:, ds(t * D + h * P, P)], ACT.Identity,
                                                bias=bn_s[:, 3, h:h + 1], scale=bn_s[:, 2, h:h + 1])
                last.then_inc(psem(phase, what), 1)

            def root(out_, in_, n):
                act.wait_ge(ln_var, n)
                nc.scalar.activation(out_, in_, ACT.Sqrt).then_inc(ln_std, 1)

            def stage_indices(n, features=False):
                which, name, weighted, counted, edges = AGGS[n]

                def stage_batch(i, g):
                    at = i * RING + g * BATCH
                    if edges:
                        hold(act, msg_added, i * (RING // BATCH) + g + 1)
                    else:
                        hold(act, summed, at + BATCH + n * C)
                    if features:
                        edge_features(act, i, g * BATCH + BATCH - 1)
                    last = nc.scalar.copy(idx_ring[:, g * BATCH:(g + 1) * BATCH], rec_v[:, ds(at, BATCH), 0])
                    if edges:
                        last = nc.scalar.copy(eid_ring[:, g * BATCH:(g + 1) * BATCH], rec_v[:, ds(at, BATCH), 2])
                    last.then_inc(idx_ready, 1)

                def relu_batch(i, g):
                    act.wait_ge(msg_added, (i + 1) * (RING // BATCH) + g + 1)
                    half = M[:, g * BATCH % MSGS:g * BATCH % MSGS + BATCH, :]
                    nc.scalar.activation(half, half, ACT.Relu).then_inc(msg_relu, 1)

                if not edges:
                    with act.Fori(0, C // RING) as i:
                        for g in range(RING // BATCH):
                            stage_batch(i, g)
                    return
                for g in range(RING // BATCH - 1):
                    stage_batch(0, g)
                with act.Fori(0, C // RING - 1) as i:
                    for g in range(RING // BATCH):
                        ahead = g + RING // BATCH - 1
                        stage_batch(i + ahead // (RING // BATCH), ahead % (RING // BATCH))
                        relu_batch(i, g)
                i = C // RING - 1
                stage_batch(i, RING // BATCH - 1)
                for g in range(RING // BATCH):
                    relu_batch(i, g)

            def copy_weights(n, before):
                for q in range(n):
                    act.wait_ge(w_turned, before + q + 1)
                    nc.scalar.copy(wt["abcd"[q]][:, :, :].rearrange("p h d -> p (h d)"), bank[4 + q % 2][:, :])\
                      .then_inc(w_copied, 1)

            copy_weights(4, 0)
            barrier(act, 1)

            act.wait_ge(psem("records", "stored"), 1)
            take_records(act, "act")
            def split_parts(phase, src):
                def first(t, s, used):
                    act.wait_ge(*after(phase, "rows", t + 1))
                    if used:
                        hold(act, *after(phase, f"written{s}", (t - s) * (16 // PSLOTS)))
                    nc.scalar.copy(parts[:, s, 0, :], src(t, s)).then_inc(psem(phase, "first"), 1)

                def second(t, s, used):
                    act.wait_ge(*after(phase, "left", t + 1))
                    nc.scalar.copy(parts[:, s, 1, :], rest[:, s % 2, :]).then_inc(psem(phase, "second"), 1)
                return first, second

            def y_keep(t, s, used):
                hold(act, psem("y", "product"), t + 1)
                for h in range(DH):
                    last = nc.scalar.activation(H[:, ds(t * D + h * P, P)], bank[6 + s][:, h * P:(h + 1) * P],
                                                ACT.Identity, bias=pcol[:, 0, h:h + 1])
                last.then_inc(psem("y", "kept"), 1)
            over_tiles(act, (lambda t, s, used: copy_turned("y", s, t, used, "product", bank[4 + s]), 0), (y_keep, 1))
            root(bn_s[:, 1, :], bn_s[:, 0, :], 1)
            act.wait_ge(vars_in, 1)
            first, second = split_parts("h", lambda t, s: nm[:, s % 2, :])
            over_tiles(act, (lambda t, s, used: normed("h", t, s, used, "turned", "scaled"), 0), (first, 1, PSLOTS), (second, 2, PSLOTS))
            barrier(act, 2)
            barrier(act, 3)
            barrier(act, 4)
            stage_indices(0)
            barrier(act, 5)

            def conv_in(t, s, used):
                copy_turned("conv", s, t, used, "mid", bank[0 + s])
                normed("conv", t, s, used, "mid", "hT")

            def conv_gelu(t, s, used):
                act.wait_ge(psem("conv", "mid"), t + 1)
                if used:
                    hold(act, psem("conv", "product"), t - 1)
                for h in range(DH):
                    last = nc.scalar.activation(gT[:, s, h * P:(h + 1) * P], bank[2 + s][:, h * P:(h + 1) * P],
                                                ACT.Gelu, bias=pcol[:, 3, h:h + 1])
                last.then_inc(psem("conv", "gT"), 1)
            over_tiles(act, (conv_in, 0), (conv_gelu, 1))
            root(bn_s[:, 1, :], bn_s[:, 0, :], 2)
            act.wait_ge(vars_in, 2)
            over_tiles(act, lambda t, s, used: normed("z", t, s, used, "turned", "scaled"))
            barrier(act, 6)
            root(std[:, :], rstd[:, :], 3)
            root(dis[:, :], dis_r[:, :], 4)
            barrier(act, 7)
            stage_indices(1)
            barrier(act, 8)
            over_tiles(act, lambda t, s, used: copy_turned("lin1", s, t, used, "product", bank[0 + s]))
            barrier(act, 9)
            root(std[:, :], rstd[:, :], 5)
            first, second = split_parts("ln1", lambda t, s: tile(H, t))
            over_tiles(act, (first, 0, PSLOTS), (second, 1, PSLOTS))
            barrier(act, 10)
            stage_indices(2)
            barrier(act, 11)

            def gcn_stages(phase):
                def gelu(t, s, used):
                    act.wait_ge(*after(phase, "taken", t + 1))
                    if used:
                        hold(act, *after(phase, "rows", t - 1))
                    nc.scalar.activation(hT[:, s, :], gT[:, s, :], ACT.Gelu_apprx_tanh).then_inc(psem(phase, "gelu"), 1)
                first, second = split_parts(phase, lambda t, s: tile(H, t))
                return ((lambda t, s, used: copy_turned(phase, s, t, used, "product", bank[0 + s]), 0), (gelu, 2),
                        (first, 3, PSLOTS), (second, 4, PSLOTS))
            over_tiles(act, *gcn_stages("gcn0"))
            barrier(act, 12)
            stage_indices(3)
            barrier(act, 13)
            over_tiles(act, *gcn_stages("gcn1"))
            barrier(act, 14)
            stage_indices(4)
            barrier(act, 15)
            over_tiles(act, lambda t, s, used: copy_turned("gcn2", s, t, used, "product", bank[0 + s]))
            barrier(act, 16)
            root(std[:, :], rstd[:, :], 6)
            copy_weights(2, 4)
            barrier(act, 17)
            disorder = act.value_load(unsorted[0:1, 0:1], min_val=0, max_val=E)
            with act.If(disorder == 0):
                stage_indices(5, features=True)
            with act.Else():
                stage_indices(5)
            barrier(act, 18)
            root(bn_s[:, 1, :], bn_s[:, 0, :], 7)
            root(bias[:, 3, :], H[:, 3 * D:4 * D], 8)
            barrier(act, 19)

            def ffn_gelu(t, s, used):
                act.wait_ge(psem("ffn", "mid"), t + 1)
                if used:
                    hold(act, psem("ffn", "product"), t - 1)
                for h in range(DH):
                    last = nc.scalar.activation(gT[:, s, h * P:(h + 1) * P], bank[2 + s][:, h * P:(h + 1) * P],
                                                ACT.Gelu, bias=pcol[:, 0, h:h + 1])
                last.then_inc(psem("ffn", "gT"), 1)
            over_tiles(act, (lambda t, s, used: copy_turned("ffn", s, t, used, "mid", bank[0 + s], bn_s[:, 2, :],
                                                            bn_s[:, 3, :]), 0), (ffn_gelu, 1))
            barrier(act, 20)
            root(std[:, :], rstd[:, :], 9)
            barrier(act, 21)

        @block.vector
        def _(dve):
            chain = [0]
            ts, tt, stt = nc.vector.tensor_scalar, nc.vector.tensor_tensor, nc.vector.scalar_tensor_tensor

            def link(ins):
                chain[0] += 1
                ins.then_inc(vec_chain, 1)
                dve.wait_ge(vec_chain, chain[0])

            def sort(k):
                own = ("src", "dst")[k]
                link(ts(tmp_i, ends[own], 7, None, ALU.logical_shift_right))
                link(nc.vector.tensor_copy(key, tmp_i))
                if k == 1:
                    nc.vector.tensor_copy(slot_f, ends["dst"])
                    link(nc.vector.tensor_copy(scan, dst_next))
                    link(tt(mask, slot_f, scan, ALU.is_gt))
                    link(ts(mask, mask, 1.0, 0.0, ALU.mult, ALU.add, accum_out=cnt[:, 5, 3:4]))
                base = chain[0]
                with dve.Fori(0, T) as b:
                    nc.vector.tensor_scalar(mask, key, iota_row[:, ds(b, 1)], 0.0, ALU.is_equal, ALU.add,
                                            accum_out=cnt[:, 0, ds(b, 1)]).then_inc(vec_chain, 1)
                    hold(dve, vec_chain, b + (base + 1))
                chain[0] += T
                nc.vector.drain().then_inc(sorts, 1)
                dve.wait_ge(psem("sort", "mm"), 3 * k + 1)
                link(ts(cnt_i[:, 0, 0:T], bank[1][:, 0:T], float(P - 1), None, ALU.add))
                link(ts(cnt_i[:, 0, 0:T], cnt_i[:, 0, 0:T], 7, None, ALU.logical_shift_right))
                link(nc.vector.tensor_copy(cnt[:, 1, 0:T], cnt_i[:, 0, 0:T]))
                link(ts(cnt_i[0:T, 1, 0:1], bank[2][0:T, 0:1], float(P - 1), None, ALU.add))
                link(ts(cnt_i[0:T, 1, 0:1], cnt_i[0:T, 1, 0:1], 7, None, ALU.logical_shift_right))
                link(nc.vector.tensor_copy(cnt[0:T, 5, 0:1], cnt_i[0:T, 1, 0:1]))
                dve.sem_inc(sorts, 1)
                if k == 1:
                    ts(sorted_f[:, :], bank[2][:, 1:2], 0.0, None, ALU.is_equal)
                    nc.vector.tensor_copy(unsorted[:, :], bank[2][0:1, 1:2])
                    link(stt(cnt[0:T, 5, 2:3], cnt[0:T, 5, 0:1], float(P), bank[2][0:T, 0:1], ALU.mult, ALU.subtract))
                    link(ts(pad_rows[0:T, :], ones[0:T, :], cnt[0:T, 5, 2:3], None, ALU.mult))
                link(nc.vector.tensor_tensor_scan(cnt[:, 2, 0:T], cnt[:, 1, 0:T], cnt[:, 1, 0:T], 0.0, ALU.add, ALU.max))
                link(tt(cnt[:, 3, 0:T], cnt[:, 2, 0:T], cnt[:, 1, 0:T], ALU.subtract))
                link(stt(cnt[:, 4, 0:T], cnt[:, 3, 0:T], float(P), bank[0][:, 0:T], ALU.mult, ALU.add))
                dve.wait_ge(psem("sort", "mm"), 3 * k + 2)
                link(nc.vector.tensor_copy(cnt[0:T, 5, 1:2], bank[3][0:T, 0:1]))
                dve.wait_ge(psem("sort", "chunk_no"), 1)
                link(ts(chunk_cmp[0:T, :], chunk_no[0:T, :], cnt[0:T, 5, 1:2], None, ALU.is_ge))
                dve.sem_inc(sorts, 1)
                link(nc.vector.memset(slot_f, 0.0))
                base = chain[0]
                with dve.Fori(0, T) as b:
                    ts(mask, key, iota_row[:, ds(b, 1)], None, ALU.is_equal).then_inc(vec_chain, 1)
                    hold(dve, vec_chain, b * 3 + (base + 1))
                    nc.vector.tensor_tensor_scan(scan, mask, mask, cnt[:, 4, ds(b, 1)], ALU.add, ALU.max).then_inc(vec_chain, 1)
                    hold(dve, vec_chain, b * 3 + (base + 2))
                    nc.vector.copy_predicated(slot_f, mask_i, scan).then_inc(vec_chain, 1)
                    hold(dve, vec_chain, b * 3 + (base + 3))
                chain[0] += 3 * T
                link(ts(tmp_i, slot_f, -1.0, 0.0, ALU.add, ALU.max))
                link(ts(slot_f, edge_no, float(P * C - PFULL * FE), None, ALU.add))
                link(ts(scan_i, tmp_i, P - 1, None, ALU.bitwise_and))
                link(ts(tmp_i, tmp_i, 7, None, ALU.logical_shift_right))
                link(stt(scan, scan_i, float(C), tmp_i, ALU.mult, ALU.add))
                link(ts(mask, key, float(T), None, ALU.is_lt))
                link(nc.vector.copy_predicated(slot_f, mask_i, scan))
                link(nc.vector.tensor_copy(slot_i[own], slot_f))
                dve.wait_ge(psem("sort", "mm"), 3 * k + 3)
                if k == 1:
                    nc.vector.tensor_scalar(tile_base[:, 0:512], bank[0][:, 0:512], float(T - 1), float(P), ALU.min, ALU.mult)
                    nc.vector.tensor_scalar(tile_base[:, 512:C], bank[1][:, 0:C - 512], float(T - 1), float(P), ALU.min, ALU.mult)
                    stt(first_edge[:, 0:512], chunk_no[:, 0:512], float(P), bank[2][:, 0:512], ALU.mult, ALU.subtract)
                    link(stt(first_edge[:, 512:C], chunk_no[:, 512:C], float(P), bank[3][:, 0:C - 512], ALU.mult, ALU.subtract))
                    link(ts(start_row, first_edge[0:1, :], float(E - P), None, ALU.min))
                    link(ts(first_edge, first_edge, sorted_f[:, 0:1], None, ALU.mult))
                    dve.wait_ge(psem("sort", "tile_row_free"), 1)
                ts(tile_row[:, 0:512], bank[0][0:1, 0:512], float(T - 1), float(DEGW), ALU.min, ALU.mult)
                link(ts(tile_row[:, 512:C], bank[1][0:1, 0:C - 512], float(T - 1), float(DEGW), ALU.min, ALU.mult))
                dve.sem_inc(psem("sort", "tiles"), 1)

            def src_records():
                nc.vector.tensor_copy(rec_ev[:, :, 0], ends["dst"])
                nc.vector.tensor_copy(rec_ev[:, :, 2], weight)
                link(ts(tmp_i, ends["src"], P - 1, None, ALU.bitwise_and))
                link(nc.vector.tensor_copy(rec_ev[:, :, 1], tmp_i))

            def dst_records():
                nc.vector.tensor_copy(plain_ev[:, :, 0], ends["src"])
                link(nc.vector.tensor_copy(plain_ev[:, :, 1], ends["dst"]))
                dve.sem_inc(psem("sort", "records"), 1)

            def rows_in_tiles():
                before = ring_mem[:, 0:C]
                tt(before, rec_v[:, :, 2], first_edge, ALU.is_lt)
                link(tt(rec_v[:, :, 1], rec_v[:, :, 1], tile_base, ALU.subtract))
                link(stt(rec_v[:, :, 1], before, float(2 * NO_TILE), rec_v[:, :, 1], ALU.mult, ALU.add))

            def add_chunks(n):
                which, name, weighted, counted, edges = AGGS[n]
                width = DEGW if counted else D

                exact = weighted or edges

                def batch_of(i, g):
                    slot = g * BATCH % ONEHOTS
                    return (onehot if exact else onehot_bf)[:, slot:slot + BATCH, :]

                def word(w, i, g):
                    return rec_v[:, ds(i * RING + g * BATCH, BATCH), w:w + 1].to_broadcast((P, BATCH, P))

                def one_hots(i, g):
                    tt(batch_of(i, g), iota_row[:, :].unsqueeze(1).to_broadcast((P, BATCH, P)), word(1, i, g), ALU.is_equal)\
                        .then_inc(onehot_raw if weighted else onehot_ready, 1)

                def weight_one_hots(i, g):
                    dve.wait_ge(onehot_raw, i * (RING // BATCH) + g + 1)
                    tt(batch_of(i, g), batch_of(i, g), word(2, i, g), ALU.mult).then_inc(onehot_ready, 1)

                def messages(i, g):
                    dve.wait_ge(gathered[g], (i + (n * (C // RING) + 1)) * (16 * BATCH))
                    dve.wait_ge(ea_in[g], (i + 1) * (16 * BATCH))
                    at, slot = g * BATCH, g * BATCH % MSGS
                    tt(M[:, slot:slot + BATCH, :], G[:, at:at + BATCH, 0:D], EA[:, at:at + BATCH, :], ALU.add)\
                        .then_inc(msg_added, 1)

                steps = [messages, one_hots] if edges else [one_hots, weight_one_hots] if weighted else [one_hots]

                def body(i, last):
                    for s in range(RING):
                        c = i * RING + s + n * C
                        column = dve.value_load(tile_row[0:1, ds(i * RING + s, 1)], min_val=0, max_val=(T - 1) * DEGW)
                        ahead = (i + (s // BATCH * BATCH + BATCH) // RING, (s // BATCH + 1) % (RING // BATCH))
                        more = not (last and s + BATCH >= RING)
                        turn_ = c + (RING + 1)
                        dve.wait_ge(summed, turn_)
                        dve.wait_ge(added, turn_)
                        to = acc[:, ds(column, width)]
                        tt(to, bank[s % SUMS][:, 0:width], to, ALU.add).then_inc(added, 1)
                        if more and s % BATCH < len(steps):
                            steps[s % BATCH](*ahead)

                for step in steps:
                    step(0, 0)
                with dve.Fori(0, C // RING - 1) as i:
                    body(i, False)
                body(C // RING - 1, True)

            def batch_norm(n, g, b):
                for h in range(DH):
                    link(nc.vector.bn_aggr(bn_mv[:, h, :], stats[:, h, :]))
                fixed_norm(n, bn_mv[:, :, 0], bn_mv[:, :, 1], g, b)

            def fixed_norm(n, mean, var, g, b):
                link(ts(bn_s[:, 0, :], var, EPS, None, ALU.add))
                dve.sem_inc(ln_var, 1)
                dve.wait_ge(ln_std, n)
                link(nc.vector.reciprocal(bn_s[:, 1, :], bn_s[:, 1, :]))
                link(tt(bn_s[:, 2, :], bn_s[:, 1, :], g, ALU.mult))
                link(tt(bn_s[:, 3, :], mean, bn_s[:, 2, :], ALU.mult))
                link(tt(bn_s[:, 3, :], b, bn_s[:, 3, :], ALU.subtract))

            def stage_tile(phase, src, lag=0):
                def body(t, s, used):
                    if used:
                        dve.wait_ge(*after(phase, "turned", t - 1))
                    ts(stg[:, s, :], src(t), 1.0, None, ALU.mult).then_inc(psem(phase, "staged"), 1)
                return body

            def tile_stats(phase):
                def body(t, s, used):
                    hold(dve, *after(phase, "kept", t + 1))
                    n = LAST if isinstance(t, int) and t == T - 1 else P
                    for h in range(DH):
                        last = nc.vector.bn_stats(stats[:, h, ds(t * 6, 6)], H[:, ds(t * D + h * P, n)])
                    last.then_inc(psem(phase, "stats"), 1)
                return body

            def row_stats(phase):
                def body(t, s, used):
                    hold(dve, *after(phase, "v", t + 1))
                    nc.vector.bn_stats(ln_stats[:, ds(t * 6, 6)], tile(acc, t, DEGW)).then_inc(psem(phase, "row_stats"), 1)
                return body

            def third_part(t, s, used):
                dve.wait_ge(psem("h", "second"), t + 1)
                tt(parts[:, s, 2, :], rest[:, s % 2, :], parts[:, s, 1, :], ALU.subtract).then_inc(psem("h", "parts"), 1)

            def left_of(phase, src):
                def body(t, s, used):
                    dve.wait_ge(*after(phase, "first", t + 1))
                    if later(t, 2):
                        dve.wait_ge(*after(phase, "parts", t - 1))
                    tt(rest[:, s % 2, :], src(t, s % 2), parts[:, s, 0, :], ALU.subtract).then_inc(psem(phase, "left"), 1)
                return body

            def layer_norm(phase, n, scaled=False):
                st = ln_stats.rearrange("p (t c) -> p t c", c=6)
                tt(mean[:, :], st[:, :, 1], st[:, :, 4], ALU.add)
                tt(ln_w[:, 0, :], st[:, :, 1], st[:, :, 4], ALU.subtract)
                link(tt(ln_w[:, 1, :], st[:, :, 2], st[:, :, 5], ALU.add))
                ts(mean[:, :], mean[:, :], 0.5, None, ALU.mult)
                link(stt(ln_w[:, 2, :], ln_w[:, 0, :], 0.25, ln_w[:, 0, :], ALU.mult, ALU.mult))
                link(stt(rstd[:, :], ln_w[:, 1, :], 1.0 / D, ln_w[:, 2, :], ALU.mult, ALU.add))
                link(ts(rstd[:, :], rstd[:, :], EPS, None, ALU.add))
                dve.sem_inc(ln_var, 1)
                dve.wait_ge(ln_std, n)
                link(nc.vector.reciprocal(rstd[:, :], std[:, :]))
                if n == 3:
                    link(ts(dis_r[:, :], acc[:, :].rearrange("p (t d) -> p t d", d=DEGW)[:, :, D], 1.0, None, ALU.add))
                    dve.sem_inc(ln_var, 1)
                    dve.wait_ge(ln_std, n + 1)
                    link(nc.vector.reciprocal(dis[:, :], dis[:, :]))

                def normal(t, s, used):
                    ts(tile(X, t), tile(acc, t, DEGW), mean[:, ds(t, 1)], rstd[:, ds(t, 1)], ALU.subtract, ALU.mult)\
                        .then_inc(psem(phase, "x" if scaled else "rows"), 1)

                def scale(t, s, used):
                    dve.wait_ge(*after(phase, "x", t + 1))
                    ts(tile(H, t), tile(X, t), dis[:, ds(t, 1)], None, ALU.mult).then_inc(psem(phase, "rows"), 1)

                if scaled:
                    over_tiles(dve, (normal, 0), (scale, 1), (left_of(phase, lambda t, s: tile(H, t)), 3, PSLOTS))
                else:
                    over_tiles(dve, normal)
                dve.wait_ge(*after(phase, "rows", T))
                nc.vector.memset(acc[:, :], 0.0)

            nc.vector.memset(ends["dst"], NO_TILE)
            nc.vector.memset(ends["src"], NO_TILE)
            nc.vector.memset(dst_next, NO_TILE)
            nc.vector.memset(X[:, (T - 1) * D:T * D], 0.0)
            link(nc.vector.memset(weight, 0.0))
            dve.sem_inc(fills, 1)
            link(nc.vector.memset(rec[:, :], 0.0))
            link(nc.vector.memset(rec_v[:, :, 1], -1.0))
            dve.sem_inc(fills, 1)
            dve.wait_ge(constants_ready, 2)
            dve.wait_ge(edges_in, 128)
            dve.wait_ge(psem("sort", "padded"), 1)
            sort(0)
            src_records()
            barrier(dve, 1)

            sort(1)
            dst_records()
            over_tiles(dve, (stage_tile("y", lambda t: tile(X, t)), 0), (tile_stats("y"), 2))
            dve.wait_ge(psem("y", "stats"), T)
            batch_norm(1, pcol[:, 1, :], pcol[:, 2, :])
            dve.sem_inc(vars_in, 1)

            def h_tile(t, s, used):
                if used:
                    dve.wait_ge(psem("h", "left"), t - 1)
                hold(dve, psem("h", "turned"), t + 1)
                nc.vector.tensor_copy(nm[:, s, :], bank[2 + s][:, 0:D]).then_inc(psem("h", "rows"), 1)
            over_tiles(dve, (h_tile, 0), (left_of("h", lambda t, s: nm[:, s, :]), 1, PSLOTS), (third_part, 2, PSLOTS))
            barrier(dve, 2)
            barrier(dve, 3)
            rows_in_tiles()
            barrier(dve, 4)
            nc.vector.memset(GP[:, :, PARTS * D], 1.0)
            link(nc.vector.memset(acc[:, :], 0.0))
            dve.sem_inc(summed, RING)
            dve.sem_inc(added, RING + 1)
            add_chunks(0)
            barrier(dve, 5)

            def conv_keep(t, s, used):
                dve.wait_ge(psem("conv", "product"), t + 1)
                for h in range(DH):
                    last = ts(H[:, ds(t * D + h * P, P)], bank[4 + s][:, h * P:(h + 1) * P], pcol[:, 4, h:h + 1], None, ALU.add)
                last.then_inc(psem("conv", "kept"), 1)
            over_tiles(dve, (stage_tile("conv", lambda t: tile(acc, t, DEGW)), 0), (conv_keep, 3), (tile_stats("conv"), 4))
            dve.wait_ge(psem("conv", "stats"), T)
            batch_norm(2, pcol[:, 5, :], pcol[:, 6, :])
            dve.sem_inc(vars_in, 1)

            def z_tile(t, s, used):
                dve.wait_ge(psem("z", "turned"), t + 1)
                stt(tile(acc, t, DEGW), tile(X, t), 2.0, bank[6 + s][:, 0:D], ALU.mult, ALU.add).then_inc(psem("z", "v"), 1)
            over_tiles(dve, (z_tile, 0), (row_stats("z"), 1))
            barrier(dve, 6)
            layer_norm("ln0", 3)
            barrier(dve, 7)
            add_chunks(1)
            barrier(dve, 8)

            def lin1_add(t, s, used):
                dve.wait_ge(psem("lin1", "product"), t + 1)
                tt(tile(acc, t, DEGW), bank[2 + s][:, 0:D], tile(X, t), ALU.add).then_inc(psem("lin1", "v"), 1)
            over_tiles(dve, (stage_tile("lin1", lambda t: tile(acc, t, DEGW)), 0), (lin1_add, 2), (row_stats("lin1"), 3))
            barrier(dve, 9)
            layer_norm("ln1", 5, scaled=True)
            barrier(dve, 10)
            add_chunks(2)
            barrier(dve, 11)

            def gcn_stage(phase):
                def body(t, s, used):
                    if used:
                        dve.wait_ge(*after(phase, "turned", t - 1))
                    tt(stg[:, s, :], tile(acc, t, DEGW), tile(H, t), ALU.add).then_inc(psem(phase, "staged"), 1)
                return body

            def gcn_bias(phase, i, reader):
                def body(t, s, used):
                    dve.wait_ge(*after(phase, "product", t + 1))
                    if used:
                        dve.wait_ge(*after(phase, reader, t - 1))
                    stt(gT[:, s, :], bank[2 + s][:, 0:D], dis[:, ds(t, 1)], bias[:, i, :], ALU.mult, ALU.add)\
                        .then_inc(psem(phase, "taken"), 1)
                return body

            def gcn_rows(phase):
                def body(t, s, used):
                    dve.wait_ge(*after(phase, "gelu", t + 1))
                    ts(tile(H, t), hT[:, s, :], dis[:, ds(t, 1)], None, ALU.mult).then_inc(psem(phase, "rows"), 1)
                return body

            def gcn_layer(phase, i):
                over_tiles(dve, (gcn_stage(phase), 0), (gcn_bias(phase, i, "gelu"), 2), (gcn_rows(phase), 3),
                           (left_of(phase, lambda t, s: tile(H, t)), 4, PSLOTS))

            gcn_layer("gcn0", 0)
            link(nc.vector.memset(acc[:, :], 0.0))
            barrier(dve, 12)
            add_chunks(3)
            barrier(dve, 13)
            gcn_layer("gcn1", 1)
            link(nc.vector.memset(acc[:, :], 0.0))
            barrier(dve, 14)
            add_chunks(4)
            barrier(dve, 15)

            def gcn2_add(t, s, used):
                dve.wait_ge(*after("gcn2", "taken", t + 1))
                tt(tile(acc, t, DEGW), gT[:, s, :], tile(X, t), ALU.add).then_inc(psem("gcn2", "v"), 1)
            over_tiles(dve, (gcn_stage("gcn2"), 0), (gcn_bias("gcn2", 2, "v"), 2), (gcn2_add, 3), (row_stats("gcn2"), 4))
            barrier(dve, 16)
            layer_norm("ln2", 6)
            barrier(dve, 17)
            dve.sem_inc(msg_added, RING // BATCH)
            add_chunks(5)
            barrier(dve, 18)
            fixed_norm(7, pcol[:, 3, :], pcol[:, 4, :], pcol[:, 1, :], pcol[:, 2, :])
            dve.wait_ge(psem("norm2", "in"), 16 * 4)
            link(ts(H[:, 3 * D:4 * D], H[:, 3 * D:4 * D], EPS, None, ALU.add))
            dve.sem_inc(ln_var, 1)
            dve.wait_ge(ln_std, 8)
            link(nc.vector.reciprocal(bias[:, 3, :], bias[:, 3, :]))
            link(tt(bias[:, 1, :], bias[:, 3, :], H[:, 0:D], ALU.mult))
            link(tt(bias[:, 2, :], H[:, 2 * D:3 * D], bias[:, 1, :], ALU.mult))
            link(tt(bias[:, 2, :], H[:, D:2 * D], bias[:, 2, :], ALU.subtract))
            barrier(dve, 19)

            def ffn_stage(t, s, used):
                if used:
                    dve.wait_ge(psem("ffn", "turned"), t - 1)
                stt(stg[:, s, :], tile(X, t), 2.0, tile(acc, t, DEGW), ALU.mult, ALU.add).then_inc(psem("ffn", "staged"), 1)
                dve.wait_ge(psem("ffn", "staged"), t + 1)
                ts(tile(acc, t, DEGW), stg[:, s, :], 1.0, None, ALU.mult).then_inc(psem("ffn", "h"), 1)

            def ffn_add(t, s, used):
                dve.wait_ge(psem("ffn", "product"), t + 1)
                dve.wait_ge(psem("ffn", "h"), t + 1)
                if used:
                    dve.wait_ge(psem("ffn", "scaled"), t - 1)
                tt(nm[:, s, :], bank[4 + s][:, 0:D], tile(acc, t, DEGW), ALU.add).then_inc(psem("ffn", "taken"), 1)

            def ffn_scale(t, s, used):
                dve.wait_ge(psem("ffn", "taken"), t + 1)
                if used:
                    dve.wait_ge(psem("ffn", "v"), t - 1)
                tt(rest[:, s, :], nm[:, s, :], bias[:, 1, :], ALU.mult).then_inc(psem("ffn", "scaled"), 1)

            def ffn_shift(t, s, used):
                dve.wait_ge(psem("ffn", "scaled"), t + 1)
                tt(rest[:, s, :], rest[:, s, :], bias[:, 2, :], ALU.add).then_inc(psem("ffn", "shifted"), 1)

            def ffn_v(t, s, used):
                dve.wait_ge(psem("ffn", "shifted"), t + 1)
                tt(tile(acc, t, DEGW), rest[:, s, :], tile(X, t), ALU.add).then_inc(psem("ffn", "v"), 1)
            over_tiles(dve, (ffn_stage, 0), (ffn_add, 3), (ffn_scale, 4), (ffn_shift, 5), (ffn_v, 5), (row_stats("ffn"), 6))
            barrier(dve, 20)
            layer_norm("ln3", 9)
            barrier(dve, 21)


_INS = ["x", "src", "dst", "edge_attr_256", "edge_weight",
        "L0_gnn_w1", "L0_gnn_b1", "L0_gnn_g1", "L0_gnn_beta1", "L0_gnn_wr", "L0_gnn_br", "L0_gnn_wroot",
        "L0_gnn_w2", "L0_gnn_b2", "L0_gnn_g2", "L0_gnn_beta2", "L1_gnn_W", "L1_gnn_b",
        "L2_gnn_W1", "L2_gnn_b1", "L2_gnn_W2", "L2_gnn_b2", "L2_gnn_W3", "L2_gnn_b3",
        "L3_gnn_W1", "L3_gnn_b1", "L3_gnn_W2", "L3_gnn_b2",
        "L3_gnn_bn1_gamma", "L3_gnn_bn1_beta", "L3_gnn_bn1_mean", "L3_gnn_bn1_var",
        "L3_gnn_bn2_gamma", "L3_gnn_bn2_beta", "L3_gnn_bn2_mean", "L3_gnn_bn2_var"]


def kernel(**inputs):
    import numpy as _np
    import concourse.bacc as _bacc
    from concourse import mybir as _mybir
    from concourse.bass_utils import run_bass_kernel_spmd as _run

    nc = _bacc.Bacc("TRN2", target_bir_lowering=False, num_devices=1)
    arrays, args = {}, {}
    for name in _INS:
        arr = _np.ascontiguousarray(inputs[name])
        arrays[f"in_{name}_dram"] = arr
        args[name] = nc.dram_tensor(f"in_{name}_dram", arr.shape, _mybir.dt.from_np(arr.dtype), kind="ExternalInput").ap()
    n, d = inputs["x"].shape
    out = nc.dram_tensor("out_0_dram", (n, d), _mybir.dt.float32, kind="ExternalOutput").ap()
    gnn_kernel(nc, args, out)
    r = _run(nc, [arrays], core_ids=[0])
    return r.results[0]["out_0_dram"]
```
